# Optimizing a Trainium2 kernel written in Bass

```python
import numpy as np
import jax
import jax.numpy as jnp

def _softmax(x, axis=-1):
    return jax.nn.softmax(x, axis=axis)

def _gelu(x):
    return jax.nn.gelu(x, approximate=True)

def _silu(x):
    return jax.nn.silu(x)

def _sigmoid(x):
    return jax.nn.sigmoid(x)

def _layernorm(x, axis=-1, eps=1e-05):
    m = jnp.mean(x, axis=axis, keepdims=True)
    v = jnp.var(x, axis=axis, keepdims=True)
    return (x - m) / jnp.sqrt(v + eps)

def _scatter_add(tgt, idx, src, axis=0):
    return tgt.at[idx].add(src)

def _segment_sum(src, seg, n):
    return jax.ops.segment_sum(src, seg, n)
kernel_name = 'mk_cond_resid_d2_seqx_r2_4a87ed'

def setup_inputs(seed: int=0):
    np.random.seed(seed)
    _w = jnp.asarray

    def _rec_inputs():
        import jax
        import jax.numpy as jnp
        _rk = jax.random.key(seed)
        x = -0.000125 + 0.9999 * jax.random.normal(jax.random.fold_in(_rk, 1), (4, 1024, 512), jnp.float32)
        _lenS = 1024 - jax.random.randint(jax.random.fold_in(_rk, 7), (4,), 0, max(1, 1024 // 4) + 1, jnp.int32)
        _lenS2 = 1024 - jax.random.randint(jax.random.fold_in(_rk, 8), (4,), 0, max(1, 1024 // 4) + 1, jnp.int32)
        cond_1024 = 0.00513981 + 1.0024 * jax.random.normal(jax.random.fold_in(_rk, 11), (4, 512), jnp.float32)
        return (x, cond_1024)
    x, cond_1024 = _rec_inputs()

    def _L0_cond_setup():
        import jax, jax.numpy as jnp
        import numpy as np
        IN_FEATURES = 512
        OUT_FEATURES = 512
        BATCH = 32
        SEQ = 512
        EPS = 1e-08
        key = jax.random.key(seed)
        k1, k2, k3 = jax.random.split(key, 3)
        Efou = jax.random.normal(k1, (BATCH, SEQ, IN_FEATURES), dtype=jnp.float32)
        y = jax.random.normal(k2, (BATCH, IN_FEATURES), dtype=jnp.float32)
        weight = jax.random.normal(k3, (IN_FEATURES, OUT_FEATURES), dtype=jnp.float32)
        return {'Efou': Efou, 'y': y, 'weight': weight}
    _L0_cond_all = _L0_cond_setup()
    _L0_cond_in = {k: v for k, v in _L0_cond_all.items() if k in ('weight',)}
    del _L0_cond_all

    def _L1_cond_setup():
        import jax, jax.numpy as jnp
        import numpy as np
        D, HS, HE, E, K = (512, 1024, 512, 8, 2)
        B, T = (4, 512)
        N_SHARED = 1
        key = jax.random.key(seed)
        ks = jax.random.split(key, 9)
        g = lambda k, shape, s: jax.random.normal(k, shape, jnp.float32) * s
        return {'x': g(ks[0], (B, T, D), 1.0), 't_emb': g(ks[1], (B, D), 1.0), 'router_W': g(ks[2], (2 * D, E), 0.01), 'router_bias': jnp.zeros((E,), jnp.float32), 'w1': g(ks[3], (D, HS), 0.02), 'w3': g(ks[4], (D, HS), 0.02), 'w2': g(ks[5], (HS, D), 0.02), 'W1e': g(ks[6], (E, D, HE), 0.02), 'W2e': g(ks[7], (E, HE, D), 0.02)}
    _L1_cond_all = _L1_cond_setup()
    _L1_cond_in = {k: v for k, v in _L1_cond_all.items() if k in ('router_W', 'router_bias', 'w1', 'w3', 'w2', 'W1e', 'W2e')}
    del _L1_cond_all
    return {'x': x, 'cond_1024': cond_1024, 'L0_cond_weight': _L0_cond_in['weight'], 'L1_cond_router_W': _L1_cond_in['router_W'], 'L1_cond_router_bias': _L1_cond_in['router_bias'], 'L1_cond_w1': _L1_cond_in['w1'], 'L1_cond_w3': _L1_cond_in['w3'], 'L1_cond_w2': _L1_cond_in['w2'], 'L1_cond_W1e': _L1_cond_in['W1e'], 'L1_cond_W2e': _L1_cond_in['W2e']}

def reference(x, cond_1024, L0_cond_weight, L1_cond_router_W, L1_cond_router_bias, L1_cond_w1, L1_cond_w3, L1_cond_w2, L1_cond_W1e, L1_cond_W2e):
    import jax
    import jax.numpy as jnp

    def _L0_cond_ref(Efou, y, weight):
        import jax, jax.numpy as jnp
        import numpy as np
        IN_FEATURES = 512
        OUT_FEATURES = 512
        BATCH = 32
        SEQ = 512
        EPS = 1e-08
        scale = 1.0 / np.sqrt(np.float32(weight.shape[0]))
        ys = y * scale
        d = jax.lax.rsqrt(jnp.einsum('bi,io->bo', ys * ys, weight * weight) + EPS)
        out = jnp.einsum('bsi,io->bso', Efou * ys[:, None, :], weight) * d[:, None, :]
        return out

    def _L1_cond_ref(x, t_emb, router_W, router_bias, w1, w3, w2, W1e, W2e):
        import jax, jax.numpy as jnp
        import numpy as np
        D, HS, HE, E, K = (512, 1024, 512, 8, 2)
        B, T = (4, 512)
        N_SHARED = 1
        Bb, Tt, C = x.shape
        xf = x.reshape(-1, C)
        tf = jnp.broadcast_to(t_emb[:, None, :], (Bb, Tt, C)).reshape(-1, C)
        N = xf.shape[0]
        shared = jax.nn.silu(xf @ w1) * (xf @ w3) @ w2
        s = jax.nn.sigmoid((jnp.concatenate([xf, tf], axis=-1) @ router_W).astype(jnp.float32))
        sel_scores = s + router_bias
        _, topk_idx = jax.lax.top_k(sel_scores, K)
        s_sel = jnp.take_along_axis(s, topk_idx, axis=1)
        denom = s_sel.sum(axis=1, keepdims=True)
        gates = jnp.where(denom > 1e-09, s_sel / (denom + 1e-09), 1.0 / K).astype(x.dtype)
        combine = jnp.zeros((N, E), x.dtype).at[jnp.arange(N)[:, None], topk_idx].add(gates)
        h = jax.nn.gelu(jnp.einsum('nc,ech->enh', xf, W1e), approximate=False)
        y = jnp.einsum('enh,ehc->enc', h, W2e)
        routed = jnp.einsum('ne,enc->nc', combine, y)
        return ((shared + routed) / (N_SHARED + K)).reshape(Bb, Tt, C)
    x = x + _L0_cond_ref(x, cond_1024, L0_cond_weight)
    x = x + _L1_cond_ref(x, cond_1024, L1_cond_router_W, L1_cond_router_bias, L1_cond_w1, L1_cond_w3, L1_cond_w2, L1_cond_W1e, L1_cond_W2e)
    return x

_drawn_inputs = setup_inputs


def setup_inputs(seed=0):
    import zlib

    import numpy as np

    out = dict(_drawn_inputs(seed))
    spreads = {'L1_cond_router_bias': (0.0, 0.769)}
    factors = {'L1_cond_router_W': 19.985}
    for name, (base, spread) in spreads.items():
        noise = np.random.default_rng([zlib.crc32(name.encode()), seed]).standard_normal(out[name].shape)
        drawn = base * np.exp(spread * noise) if base else spread * noise
        out[name] = jnp.asarray(drawn.astype(out[name].dtype))
    for name, factor in factors.items():
        out[name] = (out[name] * factor).astype(out[name].dtype)
    return out
```

```python
import numpy as np

import concourse.bass as bass
from concourse import mybir
from concourse.alu_op_type import AluOpType as ALU
from contextlib import ExitStack

FP32 = mybir.dt.float32
FP32R = mybir.dt.float32r
INT32 = mybir.dt.int32
ACT = mybir.ActivationFunctionType
AX = mybir.AxisListType

P = 128
BATCH, SEQ, D = 4, 1024, 512
TOK = BATCH * SEQ
DC = D // P
HS = 1024
HC = HS // P
HE = 512
E = 8
K = 2
BLK = 512
NBLK = TOK // BLK
SUB = BLK // P
NT = TOK // P
RING = 4
TILES = -(-(K * TOK // P + E - 1) // RING) * RING
SLOTS = TILES * P
PADROWS = P
EPS = 1e-8
THIRD = 1.0 / 3.0
W_BATCHES = 12
KIB = 1024

C_ID, C_TRI, C_ONE, C_THR, C_REV, C_TIX, C_END = 0, 128, 256, 384, 416, 424, 424 + TILES


def shared_moe_kernel(nc, xT, w0, condT, router_w, router_b, shared_w, expert_w, consts, tokid, padslots, padrows, out):
    ctx = ExitStack()
    with ctx:
        base = -(-nc.sbuf_base // 128) * 128

        def sb(name, shape, dt, kib):
            return nc.alloc_sbuf_tensor_at(name, [P] + shape, dt, offset=base + int(kib * KIB))

        def sem(name):
            return ctx.enter_context(nc.semaphore(name))

        x1t = sb("x1t", [2, DC, BLK], FP32, 0)
        w13h = sb("w13h", [HC, 2, DC, P], FP32R, 16)
        w13l = sb("w13l", [HC, 2, DC, P], FP32R, 48)
        wmh = sb("wmh", [2, DC, D], FP32R, 80)
        wml = sb("wml", [2, DC, D], FP32R, 96)
        w2h = wmh[:, :, :, :].rearrange("p b c n -> p (b c) n")
        w2l = wml[:, :, :, :].rearrange("p b c n -> p (b c) n")
        xin = sb("xin", [2, DC, BLK], FP32, 112)
        we = sb("we", [E, 2, DC, D], FP32, 0)
        xh = sb("xh", [2, DC, BLK], FP32R, 128)
        xl = sb("xl", [2, DC, BLK], FP32R, 144)
        xg = sb("xg", [RING, D], FP32, 128)
        xgt = sb("xgt", [2, DC, P], FP32, 136)
        hid = sb("hid", [2, HE], FP32, 140)
        hidt = sb("hidt", [2, DC, P], FP32, 144)
        ys = sb("ys", [RING, D], FP32, 148)
        x1tok = sb("x1tok", [2, SUB, D], FP32, 160)
        w0sq = sb("w0sq", [DC, D], FP32, 160)
        xres = sb("xres", [SUB, D], FP32, 160)
        outst = sb("outst", [SUB, D], FP32, 168)
        condb = sb("condb", [DC, BATCH, P], FP32, 176)
        gh = sb("gh", [2, BLK], FP32R, 176)
        gl = sb("gl", [2, BLK], FP32R, 180)
        w0s = sb("w0s", [DC, D], FP32, 184)
        sil = sb("sil", [2, BLK], FP32, 184)
        gm = sb("gm", [2, BLK], FP32, 188)
        wraw = sb("wraw", [2, 1024], FP32, 192)
        rt = sb("rt", [8, NT * E], FP32, 192)
        at = [200.0]

        def small(name, shape, dt=FP32):
            n = 1
            for s in shape:
                n *= s
            t = sb(name, shape, dt, at[0])
            at[0] += -(-n * 4 // 32) * 32 / KIB
            assert base + at[0] * KIB <= nc.sbuf_usable_end
            return t

        cst = small("cst", [C_END])
        ident, tri, ones = cst[:, C_ID:C_ID + P], cst[:, C_TRI:C_TRI + P], cst[:, C_ONE:C_ONE + P]
        rw = small("rw", [2 * DC, E])
        rb = small("rb", [E])
        cnd = small("cnd", [DC, BATCH])
        mod = small("mod", [DC, BATCH])
        modsq = small("modsq", [DC, BATCH])
        dvar = small("dvar", [DC, BATCH])
        dtmp = small("dtmp", [DC, BATCH])
        dsc = small("dsc", [DC, BATCH])
        rconst = small("rconst", [BATCH, E])
        score = small("score", [NT, E])
        tid = small("tid", [NT], INT32)
        rec = small("rec", [K, NT, 2], INT32)
        sadr = small("sadr", [K, NT], INT32)
        slot = small("slot", [TILES, 2], INT32)
        etab = small("etab", [TILES], INT32)
        e8 = small("e8", [6, E])
        s32 = small("s32", [8, NT])
        gix = [small(f"gix{k}", [1], INT32) for k in range(RING)]
        six = [small(f"six{k}", [1], INT32) for k in range(RING)]

        bank = [ctx.enter_context(nc.psum_tensor(f"bank{i}", [P, 512], FP32)) for i in range(8)]
        lin_ps, tok_ps, misc_ps, logit_ps = bank[0:2], bank[2:4], bank[6], bank[7]
        a_ps, b_ps, o_ps = bank[0:2], bank[2:4], bank[4:8]
        rank_ps = bank[0]
        xt_ps, ht_ps, h_ps, y_ps = bank[0:2], bank[2:4], bank[4:6], bank[6:8]

        x1t_d = nc.dram_tensor("x1t_d", [NBLK, P, DC, BLK], FP32)
        x1_d = nc.dram_tensor("x1_d", [TOK + PADROWS, D], FP32)
        slots_d = nc.dram_tensor("slots_d", [SLOTS, 2], INT32)

        small_in = sem("small_in")
        cond_in, w0_in = sem("cond_in"), sem("w0_in")
        pads_in = sem("pads_in")
        xin_in = [sem(f"xin_in{j}") for j in range(2)]
        wraw_in = [sem(f"wraw_in{j}") for j in range(2)]
        xh_ready, xl_ready = sem("xh_ready"), sem("xl_ready")
        wmh_ready, wml_ready = sem("wmh_ready"), sem("wml_ready")
        prep = sem("prep")
        misc_done = sem("misc_done")
        root = sem("root")
        lin_done = sem("lin_done")
        x1t_done = sem("x1t_done")
        tok_done = sem("tok_done")
        x1_done = sem("x1_done")
        x1t_out = [sem(f"x1t_out{j}") for j in range(2)]
        x1_out = [sem(f"x1_out{j}") for j in range(2)]
        w_high, w_split = sem("w_high"), sem("w_split")
        logit_done, score_done = sem("logit_done"), sem("score_done")
        ab_done, sil_done = sem("ab_done"), sem("sil_done")
        gm_done = sem("gm_done")
        gh_ready, gl_ready = sem("gh_ready"), sem("gl_ready")
        down_done, o_done = sem("down_done"), sem("o_done")
        xres_in, out_stored = sem("xres_in"), sem("out_stored")
        step = sem("step")
        mask_done, rank_mm, rank_done = sem("mask_done"), sem("rank_mm"), sem("rank_done")
        sadr_done, listed, slots_in, etab_done = sem("sadr_done"), sem("listed"), sem("slots_in"), sem("etab_done")
        we_in = [sem(f"we_in{e}") for e in range(E)]
        experts_in = sem("experts_in")
        issue = sem("issue")
        ixc = sem("ixc")
        gathered = [sem(f"gathered{k}") for k in range(RING)]
        tx_done, th_done, mm1_done, mm2_done = sem("tx_done"), sem("th_done"), sem("mm1_done"), sem("mm2_done")
        xgt_done, hid_done, hidt_done = sem("xgt_done"), sem("hid_done"), sem("hidt_done")
        ys_done = sem("ys_done")
        added = sem("added")

        block = ctx.enter_context(nc.Block())

        @block.sync
        def _(sp):
            for j in range(2):
                sp.sem_inc(x1t_out[j], 16)
                sp.sem_inc(x1_out[j], 16)
            sp.dma_start(cnd[:, :, :], condT).then_inc(cond_in, 16)
            sp.dma_start(w0s[:, :, :], w0).then_inc(w0_in, 16)
            sp.dma_start(rw[:, :, :], router_w).then_inc(small_in, 16)
            sp.dma_start(xin[:, 0], xT[0]).then_inc(xin_in[0], 16)
            sp.dma_start(cst[:, :], consts).then_inc(small_in, 16)
            sp.dma_start(rb[:, :], router_b).then_inc(small_in, 16)
            sp.dma_start(tid[:, :], tokid).then_inc(small_in, 16)
            sp.dma_start(xin[:, 1], xT[1]).then_inc(xin_in[1], 16)
            for j in range(2):
                sp.dma_start(wraw[:, j, :], shared_w[j]).then_inc(wraw_in[j], 16)
            sp.dma_start(slots_d[:, :].rearrange("(p t) c -> p (t c)", p=P), padslots).then_inc(pads_in, 16)
            sp.dma_start(x1_d[TOK:TOK + PADROWS, :], padrows).then_inc(pads_in, 16)
            sp.dma_start(out[TOK:TOK + PADROWS, :], padrows).then_inc(pads_in, 16)

            def swap_x(n, j, source):
                sp.wait_ge(x1t_done, 4 * n + 4 + 2)
                sp.dma_start(x1t_d[bass.ds(n, 1)].rearrange("a p c t -> p (a c) t"), x1t[:, j]).then_inc(x1t_out[j], 16)
                sp.wait_ge(xh_ready, 4 * n + 4)
                sp.dma_start(xin[:, j], source).then_inc(xin_in[j], 16)

            with sp.Fori(0, NBLK // 2 - 1) as h:
                for j in range(2):
                    n = 2 * h + j
                    swap_x(n, j, xT[bass.ds(n + 2, 1)].rearrange("a p c t -> p (a c) t"))
                    sp.wait_ge(w_split, n + 1)
                    sp.dma_start(wraw[:, j, :], shared_w[bass.ds(n + 2, 1)].rearrange("a p n -> p (a n)")).then_inc(wraw_in[j], 16)
            for j in range(2):
                n = NBLK - 2 + j
                sp.wait_ge(x1t_out[j], 16 + 16)
                swap_x(n, j, x1t_d[j])
                sp.wait_ge(w_split, n + 1)
                sp.dma_start(wraw[:, j, :], shared_w[n + 2]).then_inc(wraw_in[j], 16)
            for j in range(2):
                sp.wait_ge(w_split, NBLK + j + 1)
                sp.dma_start(wraw[:, j, :], shared_w[NBLK + 2 + j]).then_inc(wraw_in[j], 16)
            for j in range(2):
                sp.wait_ge(x1t_out[j], 16 * NBLK // 2 + 16)
                sp.wait_ge(x1_out[j], 16 * NBLK // 2 + 16)
            sp.wait_ge(tok_done, 4 * NBLK + 5)
            sp.dma_start(we[:, 0], expert_w[0]).then_inc(we_in[0], 16)

            def load_res(n):
                sp.wait_ge(o_done, 4 * n)
                sp.dma_start(xres[:, :, :], x1_d[bass.ds(n * BLK, BLK), :].rearrange("(s p) d -> p s d", p=P)).then_inc(xres_in, 16)

            def store_out(n):
                sp.wait_ge(o_done, 4 * n + 4)
                sp.dma_start(out[bass.ds(n * BLK, BLK), :].rearrange("(s p) d -> p s d", p=P), outst[:, :, :]).then_inc(out_stored, 16)

            def load_x1t(n, j):
                sp.wait_ge(xh_ready, 4 * (NBLK + n + 1))
                sp.wait_ge(xl_ready, 4 * (NBLK + n + 1))
                sp.dma_start(xin[:, j], x1t_d[bass.ds(n + 2, 1)].rearrange("a p c t -> p (a c) t")).then_inc(xin_in[j], 16)

            load_x1t(0, 0)
            load_res(0)
            load_x1t(1, 1)
            store_out(0)
            load_res(1)
            with sp.Fori(1, NBLK // 2 - 1) as h:
                for j in range(2):
                    n = 2 * h + j
                    load_x1t(n, j)
                    store_out(n - 1)
                    load_res(n)
            sp.wait_ge(listed, 16 * K * NT)
            sp.dma_start(slot[:, :, :], slots_d[:, :].rearrange("(p t) c -> p t c", p=P)).then_inc(slots_in, 16)
            for n in (NBLK - 2, NBLK - 1):
                store_out(n - 1)
                load_res(n)
            sp.wait_ge(ab_done, HC * NBLK)
            sp.dma_start(we[:, 1], expert_w[1]).then_inc(we_in[1], 16)
            store_out(NBLK - 1)
            for e in range(2, E):
                sp.dma_start(we[:, e], expert_w[e]).then_inc(we_in[e], 16)
            for e in range(E):
                sp.wait_ge(we_in[e], 16)
                sp.sem_inc(experts_in, 1)
            sp.wait_ge(pads_in, 48)
            sp.wait_ge(out_stored, 16 * NBLK)
            sp.wait_ge(added, 16 * TILES)

        @block.tensor
        def _(pe):
            pe.sem_inc(lin_done, 1)
            pe.sem_inc(tok_done, 5)
            pe.wait_ge(prep, 4)
            pe.wait_ge(small_in, 64)
            for o in range(DC):
                for c in range(DC):
                    pe.matmul(misc_ps[:, o * BATCH:(o + 1) * BATCH], w0sq[:, c, o * P:(o + 1) * P], modsq[:, c, :],
                              start=(c == 0), stop=(c == DC - 1))
            for b in range(BATCH):
                for c in range(DC):
                    last = pe.matmul(misc_ps[:, 16 + b * E:16 + (b + 1) * E], condb[:, c, b, :], rw[:, DC + c, :],
                                     start=(c == 0), stop=(c == DC - 1))
            last.then_inc(misc_done, 1)

            def linear(n, wb, j):
                for o in range(DC):
                    pe.wait_ge(x1t_done, 4 * n + o + 1)
                    for c in range(DC):
                        if o == 0:
                            pe.wait_ge(xl_ready, 4 * n + c + 1)
                        w_hi, w_lo = wmh[:, wb, c, o * P:(o + 1) * P], wml[:, wb, c, o * P:(o + 1) * P]
                        pe.matmul(lin_ps[o % 2][:, :], w_hi, xh[:, j, c, :], start=(c == 0), stop=False)
                        pe.matmul(lin_ps[o % 2][:, :], w_hi, xl[:, j, c, :], start=False, stop=False)
                        last = pe.matmul(lin_ps[o % 2][:, :], w_lo, xh[:, j, c, :], start=False, stop=(c == DC - 1))
                    last.then_inc(lin_done, 1)

            def by_token(n, j):
                pe.wait_ge(x1t_done, 4 * n + DC + 2)
                for s in range(SUB):
                    pe.wait_ge(x1_done, 4 * n + s + 1)
                    for o in range(DC):
                        pe.matmul(logit_ps[:, bass.ds((n * SUB + s) * E, E)], x1t[:, j, o, s * P:(s + 1) * P], rw[:, o, :],
                                  start=(o == 0), stop=(o == DC - 1))
                    for o in range(DC):
                        last = pe.transpose(tok_ps[s % 2][:, o * P:(o + 1) * P], x1t[:, j, o, s * P:(s + 1) * P], ident)
                    last.then_inc(tok_done, 1)

            with pe.Fori(0, NBLK // 4) as i:
                for k in range(4):
                    if k % 2 == 0:
                        pe.wait_ge(wml_ready, DC * (2 * i + k // 2 + 1))
                    linear(4 * i + k, k // 2, k % 2)
                    if k:
                        by_token(4 * i + k - 1, (k - 1) % 2)
                by_token(4 * i + 3, 1)

            def up(n, hc, j):
                q = HC * n + hc
                if hc == 0:
                    pe.wait_ge(xl_ready, 4 * (NBLK + n + 1))
                pe.wait_ge(gm_done, q + 1)
                for ps, m in ((a_ps, 0), (b_ps, 1)):
                    for c in range(DC):
                        w_hi, w_lo = w13h[:, hc, m, c, :], w13l[:, hc, m, c, :]
                        pe.matmul(ps[hc % 2][:, :], w_hi, xh[:, j, c, :], start=(c == 0), stop=False)
                        pe.matmul(ps[hc % 2][:, :], w_hi, xl[:, j, c, :], start=False, stop=False)
                        last = pe.matmul(ps[hc % 2][:, :], w_lo, xh[:, j, c, :], start=False, stop=(c == DC - 1))
                last.then_inc(ab_done, 1)

            def down(n, hc):
                q = HC * n + hc
                pe.wait_ge(gl_ready, q + 1)
                if hc == 0:
                    pe.wait_ge(o_done, 4 * n)
                k = hc % 2
                for s in range(SUB):
                    g_hi, g_lo = gh[:, k, s * P:(s + 1) * P], gl[:, k, s * P:(s + 1) * P]
                    pe.matmul(o_ps[s][:, :], g_hi, w2h[:, hc, :], start=(hc == 0), stop=False)
                    pe.matmul(o_ps[s][:, :], g_hi, w2l[:, hc, :], start=False, stop=False)
                    last = pe.matmul(o_ps[s][:, :], g_lo, w2h[:, hc, :], start=False, stop=(hc == HC - 1))
                last.then_inc(down_done, 1)

            def shared_block(n, j):
                for hc in range(HC):
                    up(n, hc, j)
                    if hc:
                        down(n, hc - 1)
                    else:
                        down(n - 1, HC - 1)

            pe.wait_ge(w_split, HC)
            pe.wait_ge(x1t_done, DC * NBLK + 2)
            pe.wait_ge(x1_done, SUB * NBLK + 2)
            up(0, 0, 0)
            pe.wait_ge(logit_done, 1)
            for hc in range(1, HC):
                up(0, hc, 0)
                pe.wait_ge(w_split, HC + 1 + (hc - 1) // 2)
                down(0, hc - 1)
            for hc in range(HC):
                up(1, hc, 1)
                if hc:
                    down(1, hc - 1)
                else:
                    down(0, HC - 1)
                if hc == 5:
                    pe.wait_ge(mask_done, 1)
                    pe.wait_ge(gm_done, HC + hc - 1 + 1 + 2)
                    pe.matmul(rank_ps[:, 0:NT * E], tri, rt[:, 4, :], start=True, stop=True)
                    pe.matmul(rank_ps[:, NT * E:2 * NT * E], ones, rt[:, 4, :], start=True, stop=True).then_inc(rank_mm, 1)
                    pe.wait_ge(rank_done, 1)
            with pe.Fori(1, NBLK // 2) as h:
                for j in range(2):
                    shared_block(2 * h + j, j)
            down(NBLK - 1, HC - 1)

            def transpose_x(t, k, turn):
                pe.wait_ge(gathered[k % RING], 16 * turn + 16)
                pe.wait_ge(xgt_done, t + 1)
                for c in range(DC):
                    last = pe.transpose(xt_ps[k % 2][:, c * P:(c + 1) * P], xg[:, k % RING, c * P:(c + 1) * P], ident)
                last.then_inc(tx_done, 1)

            def transpose_h(t, k):
                pe.wait_ge(hid_done, t + 1 + 2)
                pe.wait_ge(hidt_done, t + 1)
                for c in range(DC):
                    last = pe.transpose(ht_ps[k % 2][:, c * P:(c + 1) * P], hid[:, k % 2, c * P:(c + 1) * P], ident)
                last.then_inc(th_done, 1)

            def expert_of(t):
                return pe.value_load(etab[0:1, bass.ds(t, 1)], min_val=0, max_val=E - 1)

            def matmul1(t, k):
                e = expert_of(t)
                pe.wait_ge(experts_in, e + 1)
                pe.wait_ge(xgt_done, t + 1 + 2)
                pe.wait_ge(hid_done, t + 1)
                for c in range(DC):
                    last = pe.matmul(h_ps[k % 2][:, :], xgt[:, k % 2, c, :],
                                     we[:, bass.ds(e, 1), 0, c, :].rearrange("p a n -> p (a n)"),
                                     start=(c == 0), stop=(c == DC - 1))
                last.then_inc(mm1_done, 1)

            def matmul2(t, k):
                e = expert_of(t)
                pe.wait_ge(hidt_done, t + 1 + 2)
                pe.wait_ge(ys_done, t + 1)
                for c in range(DC):
                    last = pe.matmul(y_ps[k % 2][:, :], hidt[:, k % 2, c, :],
                                     we[:, bass.ds(e, 1), 1, c, :].rearrange("p a n -> p (a n)"),
                                     start=(c == 0), stop=(c == DC - 1))
                last.then_inc(mm2_done, 1)

            pe.wait_ge(etab_done, 1)
            pe.wait_ge(gm_done, HC * NBLK + 2)
            transpose_x(0, 0, 0)
            pe.wait_ge(o_done, SUB * NBLK)
            matmul1(0, 0)
            transpose_x(1, 1, 0)
            transpose_h(0, 0)
            with pe.Fori(0, TILES // RING - 1) as i:
                for k in range(1, RING + 1):
                    t = RING * i + k
                    matmul1(t, k)
                    transpose_x(t + 1, k + 1, i + (k + 1) // RING)
                    matmul2(t - 1, k - 1)
                    transpose_h(t, k)
            for t in range(TILES - RING + 1, TILES):
                matmul1(t, t)
                if t + 1 < TILES:
                    transpose_x(t + 1, t + 1, (t + 1) // RING)
                matmul2(t - 1, t - 1)
                transpose_h(t, t)
            matmul2(TILES - 1, TILES - 1)

        @block.scalar
        def _(act):
            act.sem_inc(x1_done, 2)
            act.sem_inc(hid_done, 2)
            act.wait_ge(prep, 5)
            act.activation(dtmp[:, :, :], dvar[:, :, :], ACT.Sqrt).then_inc(root, 1)

            def x_high(j, c):
                act.activation(xh[:, j, c, :], xin[:, j, c, :], ACT.Copy).then_inc(xh_ready, 1)

            def weight_high(b, wb, i):
                act.wait_ge(lin_done, 4 * DC * i + 1)
                for c in range(DC):
                    act.activation(wmh[:, wb, c, :], w0s[:, c, :], ACT.Copy,
                                   scale=mod[:, c, bass.ds(b, 1)]).then_inc(wmh_ready, 1)

            def by_token(n, turn, j):
                act.wait_ge(x1_out[j], 16 * turn + 16)
                for s in range(SUB):
                    act.wait_ge(tok_done, 4 * n + s + 1 + 5)
                    act.activation(x1tok[:, j, s, :], tok_ps[s % 2][:, :], ACT.Copy).then_inc(x1_done, 1)
                act.wait_ge(x1_done, SUB * n + SUB + 2)
                act.dma_start(x1_d[bass.ds(n * BLK, BLK), :].rearrange("(s p) d -> p s d", p=P), x1tok[:, j]).then_inc(x1_out[j], 16)

            act.wait_ge(xin_in[0], 16)
            for c in range(DC):
                x_high(0, c)
            with act.Fori(0, NBLK // 4) as i:
                weight_high(2 * i, 0, i)
                for k in range(4):
                    n = 4 * i + k
                    act.wait_ge(xin_in[(k + 1) % 2], 16 * (2 * i + (k + 1) // 2) + 16)
                    act.wait_ge(lin_done, DC * n + 1)
                    for c in range(DC):
                        x_high((k + 1) % 2, c)
                    if k == 0:
                        weight_high(2 * i + 1, 1, i)
                    act.wait_ge(wraw_in[k % 2], 16 * (2 * i + k // 2) + 16)
                    act.activation(w13h[:, bass.ds(n, 1)].rearrange("p a m c n -> p (a m c n)"), wraw[:, k % 2, :],
                                   ACT.Copy).then_inc(w_high, 1)
                    if k:
                        by_token(n - 1, 2 * i + (k - 1) // 2, (k - 1) % 2)
                by_token(4 * i + 3, 2 * i + 1, 1)

            def w2_high(g):
                act.wait_ge(wraw_in[g % 2], 16 * ((HC + g) // 2) + 16)
                act.wait_ge(lin_done, DC * NBLK + 1)
                act.activation(w2h[:, 2 * g:2 * g + 2, :].rearrange("p b n -> p (b n)"), wraw[:, g % 2, :],
                               ACT.Copy).then_inc(w_high, 1)

            w2_high(0)
            act.wait_ge(logit_done, 1)
            act.activation(score[:, :, :], score[:, :, :], ACT.Sigmoid).then_inc(score_done, 1)

            def gate(n, hc):
                act.wait_ge(ab_done, HC * n + hc + 1)
                act.activation(sil[:, hc % 2, :], a_ps[hc % 2][:, :], ACT.Silu).then_inc(sil_done, 1)

            def hidden_high(n, hc):
                act.wait_ge(gm_done, HC * n + hc + 1 + 2)
                act.activation(gh[:, hc % 2, :], gm[:, hc % 2, :], ACT.Copy).then_inc(gh_ready, 1)

            def next_high(n, hc, j, turn):
                if hc == 2:
                    act.wait_ge(xin_in[(j + 1) % 2], 16 * turn + 16)
                    act.wait_ge(ab_done, HC * n)
                if 2 <= hc < 2 + DC:
                    x_high((j + 1) % 2, hc - 2)

            def block_steps(n, j, turn):
                for hc in range(HC):
                    gate(n, hc)
                    if turn is not None:
                        next_high(n, hc, j, turn)
                    hidden_high(n, hc)

            for hc in range(HC):
                gate(0, hc)
                next_high(0, hc, 0, NBLK // 2)
                hidden_high(0, hc)
                if hc in (0, 2, 4):
                    w2_high(1 + hc // 2)
            block_steps(1, 1, NBLK // 2 + 1)
            with act.Fori(1, NBLK // 2 - 1) as h:
                block_steps(2 * h, 0, NBLK // 2 + h)
                block_steps(2 * h + 1, 1, NBLK // 2 + h + 1)
            block_steps(NBLK - 2, 0, NBLK - 1)
            block_steps(NBLK - 1, 1, None)

            with act.Fori(0, TILES // 2) as i:
                for k in range(2):
                    t = 2 * i + k
                    act.wait_ge(mm1_done, t + 1)
                    act.activation(hid[:, k, :], h_ps[k][:, :], ACT.Gelu).then_inc(hid_done, 1)

        @block.vector
        def _(dve):
            steps = [0]

            def then(ins):
                steps[0] += 1
                ins.then_inc(step, 1)
                dve.wait_ge(step, steps[0])

            dve.sem_inc(x1t_done, 2)
            dve.sem_inc(gm_done, 2)
            dve.sem_inc(xgt_done, 2)
            dve.sem_inc(hidt_done, 2)
            dve.sem_inc(ys_done, 2)
            dve.wait_ge(cond_in, 16)
            dve.tensor_scalar(mod[:, :, :], cnd[:, :, :], float(np.float32(1.0) / np.sqrt(np.float32(D))), None, ALU.mult).then_inc(prep, 1)
            dve.tensor_copy(condb[:, :, :, :], cnd[:, :, :].unsqueeze(3).to_broadcast([P, DC, BATCH, P])).then_inc(prep, 1)
            dve.wait_ge(prep, 2)
            dve.tensor_tensor(modsq[:, :, :], mod[:, :, :], mod[:, :, :], ALU.mult).then_inc(prep, 1)
            dve.wait_ge(w0_in, 16)
            dve.tensor_tensor(w0sq[:, :, :], w0s[:, :, :], w0s[:, :, :], ALU.mult).then_inc(prep, 1)
            dve.wait_ge(misc_done, 1)
            dve.tensor_scalar(dvar[:, :, :].rearrange("p c b -> p (c b)"), misc_ps[:, 0:DC * BATCH], EPS, None,
                              ALU.add).then_inc(prep, 1)
            dve.tensor_copy(rconst[:, :, :].rearrange("p b e -> p (b e)"), misc_ps[:, 16:16 + BATCH * E])
            dve.wait_ge(root, 1)
            then(dve.reciprocal(dsc[:, :, :], dtmp[:, :, :]))
            then(dve.tensor_tensor(dtmp[:, :, :], dsc[:, :, :], dsc[:, :, :], ALU.mult))
            then(dve.tensor_tensor(dtmp[:, :, :], dtmp[:, :, :], dvar[:, :, :], ALU.mult))
            then(dve.tensor_scalar(dtmp[:, :, :], dtmp[:, :, :], -0.5, 1.5, ALU.mult, ALU.add))
            then(dve.tensor_tensor(dsc[:, :, :], dsc[:, :, :], dtmp[:, :, :], ALU.mult))

            def x_low(m, j, c):
                dve.wait_ge(xh_ready, DC * m + c + 1)
                dve.tensor_tensor(xl[:, j, c, :], xin[:, j, c, :], xh[:, j, c, :].bitcast(FP32), ALU.subtract).then_inc(xl_ready, 1)

            def weight_low(b, wb):
                for c in range(DC):
                    dve.wait_ge(wmh_ready, DC * b + c + 1)
                    dve.scalar_tensor_tensor(wml[:, wb, c, :], w0s[:, c, :], mod[:, c, bass.ds(b, 1)],
                                             wmh[:, wb, c, :].bitcast(FP32), ALU.mult, ALU.subtract).then_inc(wml_ready, 1)

            for c in range(DC):
                x_low(0, 0, c)
            with dve.Fori(0, NBLK // 4) as i:
                weight_low(2 * i, 0)
                for k in range(4):
                    n, j = 4 * i + k, k % 2
                    for o in range(DC):
                        dve.wait_ge(lin_done, DC * n + o + 1 + 1)
                        if o == 0:
                            dve.wait_ge(x1t_out[j], 16 * (2 * i + k // 2) + 16)
                            dve.wait_ge(tok_done, 4 * n - 4 + 5)
                        dve.scalar_tensor_tensor(x1t[:, j, o, :], lin_ps[o % 2][:, :], dsc[:, o, bass.ds(2 * i + k // 2, 1)],
                                                 xin[:, j, o, :], ALU.mult, ALU.add).then_inc(x1t_done, 1)
                        x_low(n + 1, (k + 1) % 2, o)
                    if k == 0:
                        weight_low(2 * i + 1, 1)
                    dve.wait_ge(w_high, n + 1)
                    w_hi = w13h[:, bass.ds(n, 1)].rearrange("p a m c n -> p (a m c n)").bitcast(FP32)
                    dve.tensor_tensor(w13l[:, bass.ds(n, 1)].rearrange("p a m c n -> p (a m c n)"), wraw[:, j, :],
                                      w_hi, ALU.subtract).then_inc(w_split, 1)

            def w2_low(g):
                dve.wait_ge(w_high, HC + g + 1)
                dve.tensor_tensor(w2l[:, 2 * g:2 * g + 2, :].rearrange("p b n -> p (b n)"), wraw[:, g % 2, :],
                                  w2h[:, 2 * g:2 * g + 2, :].rearrange("p b n -> p (b n)").bitcast(FP32),
                                  ALU.subtract).then_inc(w_split, 1)

            w2_low(0)
            dve.wait_ge(tok_done, 4 * NBLK + 5)
            dve.tensor_tensor(score[:, :, :].rearrange("p (b t) e -> p b t e", b=BATCH),
                              logit_ps[:, 0:NT * E].rearrange("p (b t e) -> p b t e", b=BATCH, e=E),
                              rconst[:, :, :].unsqueeze(2).to_broadcast([P, BATCH, NT // BATCH, E]), ALU.add).then_inc(logit_done, 1)

            def product(n, hc):
                dve.wait_ge(sil_done, HC * n + hc + 1)
                dve.tensor_tensor(gm[:, hc % 2, :], sil[:, hc % 2, :], b_ps[hc % 2][:, :], ALU.mult).then_inc(gm_done, 1)

            def hidden_low(n, hc):
                dve.wait_ge(gh_ready, HC * n + hc + 1)
                dve.tensor_tensor(gl[:, hc % 2, :], gm[:, hc % 2, :], gh[:, hc % 2, :].bitcast(FP32), ALU.subtract).then_inc(gl_ready, 1)

            def output(n):
                dve.wait_ge(down_done, HC * (n + 1))
                dve.wait_ge(xres_in, 16 * (n + 1))
                dve.wait_ge(out_stored, 16 * n)
                for s in range(SUB):
                    dve.scalar_tensor_tensor(outst[:, s, :], o_ps[s][:, :], THIRD, xres[:, s, :], ALU.mult, ALU.add).then_inc(o_done, 1)

            def block_step(n, hc, j, more):
                product(n, hc)
                if more and 2 <= hc < 2 + DC:
                    x_low(NBLK + n + 1, (j + 1) % 2, hc - 2)
                hidden_low(n, hc)

            def row(r, shape=(NT, E), dt=None):
                v = rt[:, r, :] if dt is None else rt[:, r, :].bitcast(dt)
                return v.rearrange("p (a b) -> p a b", b=shape[1])

            def per_tile(v):
                return v.unsqueeze(2).to_broadcast([P, NT, E])

            def per_expert(v):
                return v.unsqueeze(1).to_broadcast([P, NT, E])

            SEL, KEY, CHOICE, MASK = 0, 1, (2, 3), 4
            rev = cst[:, C_REV:C_REV + E]

            def choose(k):
                then(dve.tensor_reduce(s32[:, 0, :], row(SEL), AX.X, ALU.max))
                then(dve.tensor_tensor(row(KEY), row(SEL), per_tile(s32[:, 0, :]), ALU.is_equal))
                then(dve.tensor_tensor(row(KEY), row(KEY), per_expert(rev), ALU.mult))
                then(dve.tensor_reduce(s32[:, 0, :], row(KEY), AX.X, ALU.max))
                then(dve.tensor_tensor(row(CHOICE[k]), row(KEY), per_tile(s32[:, 0, :]), ALU.is_equal))
                then(dve.tensor_tensor(row(KEY), score[:, :, :], row(CHOICE[k]), ALU.mult))
                then(dve.tensor_reduce(s32[:, 1 + k, :], row(KEY), AX.X, ALU.add))
                if k == 0:
                    then(dve.scalar_tensor_tensor(row(SEL), row(CHOICE[0]), -3.0e38, row(SEL), ALU.mult, ALU.add))

            def gates():
                then(dve.tensor_tensor(s32[:, 3, :], s32[:, 1, :], s32[:, 2, :], ALU.add))
                then(dve.tensor_scalar(s32[:, 4, :], s32[:, 3, :], 1e-9, None, ALU.add))
                then(dve.reciprocal(s32[:, 5, :], s32[:, 4, :]))
                then(dve.tensor_scalar(s32[:, 6, :], s32[:, 3, :], 1e-9, None, ALU.is_gt))
                then(dve.tensor_scalar(s32[:, 7, :], s32[:, 6, :], -1.0 / K, 1.0 / K, ALU.mult, ALU.add))
                then(dve.tensor_tensor(s32[:, 5, :], s32[:, 5, :], s32[:, 6, :], ALU.mult))
                for k in range(K):
                    then(dve.tensor_tensor(s32[:, 1 + k, :], s32[:, 1 + k, :], s32[:, 5, :], ALU.mult))
                    then(dve.tensor_tensor(s32[:, 1 + k, :], s32[:, 1 + k, :], s32[:, 7, :], ALU.add))
                    then(dve.tensor_scalar(rec[:, k, :, 1].bitcast(FP32), s32[:, 1 + k, :], THIRD, None, ALU.mult))
                    then(dve.tensor_copy(rec[:, k, :, 0], tid[:, :]))

            WITHIN, TOTAL, PING, PONG, POS = 0, 1, 5, 6, 7

            def scan_tiles():
                src = TOTAL
                for d, dst in ((1, PING), (2, PONG), (4, PING), (8, PONG), (16, PING)):
                    dve.tensor_copy(row(dst)[:, 0:d, :], row(src)[:, 0:d, :])
                    then(dve.tensor_tensor(row(dst)[:, d:NT, :], row(src)[:, d:NT, :], row(src)[:, 0:NT - d, :], ALU.add))
                    src = dst

            def first_slots():
                count = row(PING)[:, NT - 1, :]
                then(dve.tensor_tensor(row(PONG, (E, NT)), count.unsqueeze(2).to_broadcast([P, E, NT]),
                                       cst[:, C_THR:C_THR + NT].unsqueeze(1).to_broadcast([P, E, NT]), ALU.is_gt))
                then(dve.tensor_reduce(e8[:, 0, :], row(PONG, (E, NT)), AX.X, ALU.add))
                src = 0
                for d, dst in ((1, 1), (2, 2), (4, 1)):
                    dve.tensor_copy(e8[:, dst, 0:d], e8[:, src, 0:d])
                    then(dve.tensor_tensor(e8[:, dst, d:E], e8[:, src, d:E], e8[:, src, 0:E - d], ALU.add))
                    src = dst
                then(dve.tensor_tensor(e8[:, 3, :], e8[:, 1, :], e8[:, 0, :], ALU.subtract))
                then(dve.tensor_scalar(e8[:, 4, :], e8[:, 3, :], float(P), None, ALU.mult))
                then(dve.tensor_tensor(row(POS), row(PING), row(TOTAL), ALU.subtract))
                then(dve.tensor_tensor(row(POS), row(POS), row(WITHIN), ALU.add))
                then(dve.tensor_tensor(row(POS), row(POS), per_expert(e8[:, 4, :]), ALU.add))

            def slot_rows():
                for k in range(K):
                    pos = s32[:, 3, :].bitcast(INT32)
                    tile_, part = s32[:, 4, :].bitcast(INT32), s32[:, 5, :].bitcast(INT32)
                    then(dve.tensor_tensor(row(PONG), row(CHOICE[k]), row(POS), ALU.mult))
                    then(dve.tensor_reduce(s32[:, 0, :], row(PONG), AX.X, ALU.add))
                    then(dve.tensor_copy(pos, s32[:, 0, :]))
                    then(dve.tensor_single_scalar(tile_, pos, 7, ALU.logical_shift_right))
                    then(dve.tensor_single_scalar(part, pos, P - 1, ALU.bitwise_and))
                    dve.scalar_tensor_tensor(sadr[:, k, :], part, float(TILES), tile_, ALU.mult, ALU.add).then_inc(sadr_done, 1)

            def expert_table():
                cmp_ = rt[0:1, PING:PING + 3, :].rearrange("p a b -> p (a b)")[:, 0:TILES * E].rearrange("p (t e) -> p t e", e=E)
                then(dve.tensor_tensor(cmp_, e8[0:1, 1, :].unsqueeze(1).to_broadcast([1, TILES, E]),
                                       cst[0:1, C_TIX:C_TIX + TILES].unsqueeze(2).to_broadcast([1, TILES, E]), ALU.is_le))
                etf = rt[0:1, WITHIN, 0:TILES]
                then(dve.tensor_reduce(etf, cmp_, AX.X, ALU.add))
                dve.tensor_scalar(etab[0:1, :], etf, float(E - 1), None, ALU.min).then_inc(etab_done, 1)

            for hc in range(HC):
                block_step(0, hc, 0, True)
                if hc in (0, 2, 4):
                    w2_low(1 + hc // 2)
                if hc == 5:
                    dve.wait_ge(score_done, 1)
                    then(dve.tensor_tensor(row(SEL), score[:, :, :], per_expert(rb[:, :]), ALU.add))
                if hc == 6:
                    choose(0)
                if hc == 7:
                    choose(1)
            for hc in range(HC):
                block_step(1, hc, 1, True)
                if hc == 0:
                    output(0)
                if hc == 1:
                    dve.tensor_tensor(row(MASK), row(CHOICE[0]), row(CHOICE[1]), ALU.add).then_inc(mask_done, 1)
                    gates()
                if hc == 5:
                    dve.wait_ge(rank_mm, 1)
                    then(dve.tensor_copy(rt[:, WITHIN:TOTAL + 1, :].rearrange("p a b -> p (a b)"), rank_ps[:, :]))
                    dve.sem_inc(rank_done, 1)
                    scan_tiles()
                if hc == 6:
                    first_slots()
                if hc == 7:
                    slot_rows()
                    expert_table()
            with dve.Fori(1, NBLK // 2 - 1) as h:
                for j in range(2):
                    for hc in range(HC):
                        block_step(2 * h + j, hc, j, True)
                        if hc == 0:
                            output(2 * h + j - 1)
            for n in (NBLK - 2, NBLK - 1):
                for hc in range(HC):
                    block_step(n, hc, n % 2, n < NBLK - 1)
                    if hc == 0:
                        output(n - 1)
            output(NBLK - 1)

            def take_x(t, k):
                dve.wait_ge(tx_done, t + 1)
                dve.tensor_copy(xgt[:, k % 2].rearrange("p c n -> p (c n)"), xt_ps[k % 2][:, :]).then_inc(xgt_done, 1)

            def take_h(t, k):
                dve.wait_ge(th_done, t + 1)
                dve.tensor_copy(hidt[:, k % 2].rearrange("p c n -> p (c n)"), ht_ps[k % 2][:, :]).then_inc(hidt_done, 1)

            def take_y(t, k, reused=True):
                dve.wait_ge(mm2_done, t + 1)
                if reused:
                    dve.wait_ge(added, 16 * (t + 1 - RING))
                dve.tensor_scalar(ys[:, k % RING, :], y_ps[k % 2][:, :], slot[:, bass.ds(t, 1), 1].bitcast(FP32), None,
                                  ALU.mult).then_inc(ys_done, 1)

            dve.wait_ge(slots_in, 16)
            take_x(0, 0)
            take_x(1, 1)
            take_h(0, 0)
            for t in range(1, RING + 1):
                take_x(t + 1, t + 1)
                take_y(t - 1, t - 1, False)
                take_h(t, t)
            with dve.Fori(1, TILES // RING - 1) as i:
                for k in range(1, RING + 1):
                    t = RING * i + k
                    take_x(t + 1, k + 1)
                    take_y(t - 1, k - 1)
                    take_h(t, k)
            for t in range(TILES - RING + 1, TILES):
                if t + 1 < TILES:
                    take_x(t + 1, t + 1)
                take_y(t - 1, t - 1)
                take_h(t, t)
            take_y(TILES - 1, TILES - 1)

        @block.gpsimd
        def _(pool):
            IO = bass.IndirectOffsetOnAxis
            pool.wait_ge(pads_in, 48)
            for k in range(K):
                pool.wait_ge(sadr_done, k + 1)
                for i in range(NT):
                    pool.indirect_dma_start(slots_d[:, :], IO(sadr[:, k, i:i + 1], 0), rec[:, k, i, :], None).then_inc(listed, 16)

            def gather(t, k, copies):
                pool.tensor_copy(gix[k][:, :], slot[:, bass.ds(t, 1), 0]).then_inc(ixc, 1)
                pool.wait_ge(ixc, copies)
                pool.sem_inc(issue, 1)
                pool.indirect_dma_start(xg[:, k, :], None, x1_d[:, :], IO(gix[k][:, :], 0)).then_inc(gathered[k], 16)

            def scatter(t, k, copies):
                if not isinstance(t, int) or t:
                    pool.wait_ge(added, 16 * t)
                pool.tensor_copy(six[k][:, :], slot[:, bass.ds(t, 1), 0]).then_inc(ixc, 1)
                pool.wait_ge(ys_done, t + 1 + 2)
                pool.wait_ge(ixc, copies)
                pool.sem_inc(issue, 1)
                pool.indirect_dma_start(out[:, :], IO(six[k][:, :], 0), ys[:, k, :], None,
                                        compute_op=ALU.add).then_inc(added, 16)

            pool.wait_ge(slots_in, 16)
            pool.wait_ge(ab_done, HC * NBLK)
            for t in range(RING):
                gather(t, t, t + 1)
            pool.wait_ge(out_stored, 16 * NBLK)

            def add_and_gather(t, k):
                scatter(t, k, RING + 2 * t + 1)
                pool.wait_ge(tx_done, t + 1)
                gather(t + RING, k, RING + 2 * t + 2)

            for t in range(RING):
                add_and_gather(t, t)
            with pool.Fori(1, TILES // RING - 1) as i:
                for k in range(RING):
                    add_and_gather(RING * i + k, k)
            for t in range(TILES - RING, TILES):
                scatter(t, t % RING, RING + 2 * (TILES - RING) + t - (TILES - RING) + 1)


def _by_partition(a, chunks):
    a = a.reshape(*a.shape[:-2], chunks, P, a.shape[-1])
    return np.ascontiguousarray(np.swapaxes(a, -3, -2))


def _constants():
    c = np.zeros((P, C_END), np.float32)
    c[:, C_ID:C_ID + P] = np.eye(P)
    c[:, C_TRI:C_TRI + P] = np.triu(np.ones((P, P)), 1)
    c[:, C_ONE:C_ONE + P] = 1.0
    c[:, C_THR:C_THR + NT] = P * np.arange(NT)
    c[:, C_REV:C_REV + E] = E - np.arange(E)
    c[:, C_TIX:C_TIX + TILES] = np.arange(TILES)
    tokid = (P * np.arange(NT)[None, :] + np.arange(P)[:, None]).astype(np.int32)
    pads = np.zeros((P, TILES, 2), np.int32)
    pads[:, :, 0] = TOK + np.arange(P)[:, None]
    return c, tokid, pads.reshape(P, 2 * TILES)


def kernel(**inputs):
    import concourse.bacc as bacc
    from concourse.bass_utils import run_bass_kernel_spmd

    a = {k: np.asarray(v) for k, v in inputs.items()}
    xT = a["x"].reshape(NBLK, BLK, D).transpose(0, 2, 1)
    w13 = np.stack([a["L1_cond_w1"], a["L1_cond_w3"]]).reshape(2, DC, P, HC, P).transpose(3, 2, 0, 1, 4)
    w2 = a["L1_cond_w2"].reshape(HC // 2, 2, P, D).transpose(0, 2, 1, 3)
    experts = np.stack([_by_partition(a["L1_cond_W1e"], DC), _by_partition(a["L1_cond_W2e"], DC)], axis=2)
    consts, tokid, pads = _constants()
    arrays = {
        "xT": _by_partition(xT, DC),
        "w0": _by_partition(a["L0_cond_weight"], DC),
        "condT": _by_partition(a["cond_1024"].T, DC),
        "router_w": _by_partition(a["L1_cond_router_W"], 2 * DC),
        "router_b": np.ascontiguousarray(np.broadcast_to(a["L1_cond_router_bias"], (P, E))),
        "shared_w": np.concatenate([w13.reshape(HC, P, 1024), w2.reshape(HC // 2, P, 1024)]),
        "expert_w": experts,
        "consts": consts,
        "tokid": tokid,
        "padslots": pads,
        "padrows": np.zeros((PADROWS, D), np.float32),
    }
    nc = bacc.Bacc("TRN2", target_bir_lowering=False, num_devices=1)
    args = {n: nc.dram_tensor(n, v.shape, mybir.dt.from_np(v.dtype), kind="ExternalInput").ap() for n, v in arrays.items()}
    out = nc.dram_tensor("out", (TOK + PADROWS, D), FP32, kind="ExternalOutput").ap()
    shared_moe_kernel(nc, **args, out=out)
    r = run_bass_kernel_spmd(nc, [arrays], core_ids=[0])
    return r.results[0]["out"][:TOK].reshape(BATCH, SEQ, D)
```

```python
import numpy as np

import concourse.bass as bass
from concourse import mybir
from concourse.alu_op_type import AluOpType as ALU
from contextlib import ExitStack

FP32 = mybir.dt.float32
FP32R = mybir.dt.float32r
INT32 = mybir.dt.int32
ACT = mybir.ActivationFunctionType
AX = mybir.AxisListType

P = 128
BATCH, SEQ, D = 4, 1024, 512
TOK = BATCH * SEQ
DC = D // P
HS = 1024
HC = HS // P
HE = 512
E = 8
K = 2
BLK = 512
NBLK = TOK // BLK
SUB = BLK // P
NT = TOK // P
RING = 4
TILES = -(-(K * TOK // P + E - 1) // RING) * RING
PAIR = 2
SLOTS = TILES * P
PADROWS = P
EPS = 1e-8
THIRD = 1.0 / 3.0
PIECE = 1024
HALF = DC * D
EP = E * 2 * HALF // PIECE
WRING = 4
HRING = 2 * WRING
EBLK = 2
KIB = 1024

C_ID, C_TRI, C_ONE, C_THR, C_REV, C_TIX, C_END = 0, 128, 256, 384, 416, 424, 424 + TILES


def shared_moe_kernel(nc, xT, w0, condT, router_w, router_b, shared_w, expert_w, consts, tokid, padslots, padrows, out):
    ctx = ExitStack()
    with ctx:
        base = -(-nc.sbuf_base // 128) * 128

        def sb(name, shape, dt, kib):
            return nc.alloc_sbuf_tensor_at(name, [P] + shape, dt, offset=base + int(kib * KIB))

        def sem(name):
            return ctx.enter_context(nc.semaphore(name))

        x1t = sb("x1t", [2, DC, BLK], FP32, 0)
        w13h = sb("w13h", [HC, 2, DC, P], FP32R, 16)
        w13l = sb("w13l", [HC, 2, DC, P], FP32R, 48)
        wmh = sb("wmh", [2, DC, D], FP32R, 80)
        wml = sb("wml", [2, DC, D], FP32R, 96)
        w2h = wmh[:, :, :, :].rearrange("p b c n -> p (b c) n")
        w2l = wml[:, :, :, :].rearrange("p b c n -> p (b c) n")
        xin = sb("xin", [2, DC, BLK], FP32, 144)
        we = sb("we", [WRING, 2, 2, 2, DC // 2, D], FP32R, 0)
        ehl = sb("ehl", [2, 2, PIECE], FP32R, 0)
        eraw = sb("eraw", [2, 2, PIECE], FP32, 0)
        xh = sb("xh", [2, DC, BLK], FP32R, 128)
        xl = sb("xl", [2, DC, BLK], FP32R, 112)
        xg = sb("xg", [RING, D], FP32, 144)
        xgth = sb("xgth", [2, DC, P], FP32R, 152)
        xgtl = sb("xgtl", [2, DC, P], FP32R, 156)
        hid = sb("hid", [2, HE], FP32, 128)
        hidth = sb("hidth", [2, DC, P], FP32R, 132)
        hidtl = sb("hidtl", [2, DC, P], FP32R, 136)
        ys = sb("ys", [RING, D], FP32, 176)
        xs = sb("xs", [2, PAIR, D], FP32, 192)
        x1tok = sb("x1tok", [2, SUB, D], FP32, 160)
        w0sq = sb("w0sq", [DC, D], FP32, 160)
        xres = sb("xres", [SUB, D], FP32, 160)
        outst = sb("outst", [SUB, D], FP32, 168)
        condb = sb("condb", [DC, BATCH, P], FP32, 176)
        gh = sb("gh", [2, BLK], FP32R, 176)
        gl = sb("gl", [2, BLK], FP32R, 180)
        w0s = sb("w0s", [DC, D], FP32, 184)
        sil = sb("sil", [2, BLK], FP32, 184)
        gm = sb("gm", [2, BLK], FP32, 188)
        wraw = sb("wraw", [2, 1024], FP32, 192)
        rt = sb("rt", [8, NT * E], FP32, 192)
        at = [200.0]

        def small(name, shape, dt=FP32):
            n = 1
            for s in shape:
                n *= s
            t = sb(name, shape, dt, at[0])
            at[0] += -(-n * 4 // 32) * 32 / KIB
            assert base + at[0] * KIB <= nc.sbuf_usable_end
            return t

        cst = small("cst", [C_END])
        ident, tri, ones = cst[:, C_ID:C_ID + P], cst[:, C_TRI:C_TRI + P], cst[:, C_ONE:C_ONE + P]
        rw = small("rw", [2 * DC, E])
        rb = small("rb", [E])
        cnd = small("cnd", [DC, BATCH])
        mod = small("mod", [DC, BATCH])
        modsq = small("modsq", [DC, BATCH])
        dvar = small("dvar", [DC, BATCH])
        dtmp = small("dtmp", [DC, BATCH])
        dsc = small("dsc", [DC, BATCH])
        rconst = small("rconst", [BATCH, E])
        score = small("score", [NT, E])
        tid = small("tid", [NT], INT32)
        rec = small("rec", [K, NT, 2], INT32)
        sadr = small("sadr", [K, NT], INT32)
        slot = small("slot", [TILES, 2], INT32)
        etab = small("etab", [TILES], INT32)
        eplace = small("eplace", [TILES], INT32)
        ends = small("ends", [E], INT32)
        e8 = small("e8", [6, E])
        s32 = small("s32", [8, NT])
        six = [small(f"six{k}", [1], INT32) for k in range(RING)]

        bank = [ctx.enter_context(nc.psum_tensor(f"bank{i}", [P, 512], FP32)) for i in range(8)]
        lin_ps, tok_ps, misc_ps, logit_ps = bank[0:2], bank[2:4], bank[6], bank[7]
        a_ps, b_ps, o_ps = bank[0:2], bank[2:4], bank[4:8]
        rank_ps = bank[0]
        xt_ps, h_ps, ht_ps, y_ps = bank[0:2], bank[2:4], bank[4:6], bank[6:8]

        x1t_d = nc.dram_tensor("x1t_d", [NBLK, P, DC, BLK], FP32)
        x1_d = nc.dram_tensor("x1_d", [TOK + PADROWS, D], FP32)
        xs_d = nc.dram_tensor("xs_d", [SLOTS, D], FP32)
        we_d = nc.dram_tensor("we_d", [EP, P, 2, PIECE], FP32R)
        slots_d = nc.dram_tensor("slots_d", [SLOTS, 2], INT32)

        small_in = sem("small_in")
        cond_in, w0_in = sem("cond_in"), sem("w0_in")
        pads_in = sem("pads_in")
        xin_in = [sem(f"xin_in{j}") for j in range(2)]
        wraw_in = [sem(f"wraw_in{j}") for j in range(2)]
        xh_ready, xl_ready = sem("xh_ready"), sem("xl_ready")
        wmh_ready, wml_ready = sem("wmh_ready"), sem("wml_ready")
        prep = sem("prep")
        misc_done = sem("misc_done")
        root = sem("root")
        lin_done = sem("lin_done")
        x1t_done = sem("x1t_done")
        tok_done = sem("tok_done")
        x1_done = sem("x1_done")
        x1t_out = [sem(f"x1t_out{j}") for j in range(2)]
        x1_out = [sem(f"x1_out{j}") for j in range(2)]
        w_high, w_split = sem("w_high"), sem("w_split")
        logit_done, score_done = sem("logit_done"), sem("score_done")
        ab_done, sil_done = sem("ab_done"), sem("sil_done")
        gm_done = sem("gm_done")
        gh_ready, gl_ready = sem("gh_ready"), sem("gl_ready")
        down_done, o_done = sem("down_done"), sem("o_done")
        xres_in, out_stored = sem("xres_in"), sem("out_stored")
        step = sem("step")
        mask_done, rank_mm, rank_done = sem("mask_done"), sem("rank_mm"), sem("rank_done")
        sadr_done, listed, slots_in, etab_done = sem("sadr_done"), sem("listed"), sem("slots_in"), sem("etab_done")
        er_in = [sem(f"er_in{j}") for j in range(2)]
        eh_ready, el_ready = sem("eh_ready"), sem("el_ready")
        ehl_out = [sem(f"ehl_out{j}") for j in range(2)]
        we_in = [sem(f"we_in{i}") for i in range(HRING)]
        weights_in = sem("weights_in")
        rows_in = [sem(f"rows_in{j}") for j in range(2)]
        staged = [sem(f"staged{j}") for j in range(2)]
        issue = sem("issue")
        ixc = sem("ixc")
        xg_in = [sem(f"xg_in{j}") for j in range(2)]
        tx_done, th_done, mm1_done, mm2_done = sem("tx_done"), sem("th_done"), sem("mm1_done"), sem("mm2_done")
        xgth_done, hidth_done = sem("xgth_done"), sem("hidth_done")
        xgt_done, hid_done, hidt_done = sem("xgt_done"), sem("hid_done"), sem("hidt_done")
        ys_done = sem("ys_done")
        added = sem("added")

        block = ctx.enter_context(nc.Block())

        @block.sync
        def _(sp):
            for j in range(2):
                sp.sem_inc(x1t_out[j], 16)
                sp.sem_inc(x1_out[j], 16)
                sp.sem_inc(ehl_out[j], 16)
            sp.dma_start(cnd[:, :, :], condT).then_inc(cond_in, 16)
            sp.dma_start(w0s[:, :, :], w0).then_inc(w0_in, 16)
            sp.dma_start(rw[:, :, :], router_w).then_inc(small_in, 16)
            sp.dma_start(xin[:, 0], xT[0]).then_inc(xin_in[0], 16)
            sp.dma_start(cst[:, :], consts).then_inc(small_in, 16)
            sp.dma_start(rb[:, :], router_b).then_inc(small_in, 16)
            sp.dma_start(tid[:, :], tokid).then_inc(small_in, 16)
            sp.dma_start(xin[:, 1], xT[1]).then_inc(xin_in[1], 16)
            for j in range(2):
                sp.dma_start(wraw[:, j, :], shared_w[j]).then_inc(wraw_in[j], 16)
            sp.dma_start(slots_d[:, :].rearrange("(p t) c -> p (t c)", p=P), padslots).then_inc(pads_in, 16)
            sp.dma_start(x1_d[TOK:TOK + PADROWS, :], padrows).then_inc(pads_in, 16)
            sp.dma_start(out[TOK:TOK + PADROWS, :], padrows).then_inc(pads_in, 16)

            def swap_x(n, j, source):
                sp.wait_ge(x1t_done, 4 * n + 4 + 2)
                sp.dma_start(x1t_d[bass.ds(n, 1)].rearrange("a p c t -> p (a c) t"), x1t[:, j]).then_inc(x1t_out[j], 16)
                sp.wait_ge(xh_ready, 4 * n + 4)
                sp.dma_start(xin[:, j], source).then_inc(xin_in[j], 16)

            with sp.Fori(0, NBLK // 2 - 1) as h:
                for j in range(2):
                    n = 2 * h + j
                    swap_x(n, j, xT[bass.ds(n + 2, 1)].rearrange("a p c t -> p (a c) t"))
                    sp.wait_ge(w_split, n + 1)
                    sp.dma_start(wraw[:, j, :], shared_w[bass.ds(n + 2, 1)].rearrange("a p n -> p (a n)")).then_inc(wraw_in[j], 16)
            for j in range(2):
                n = NBLK - 2 + j
                sp.wait_ge(x1t_out[j], 16 + 16)
                swap_x(n, j, x1t_d[j])
                sp.wait_ge(w_split, n + 1)
                sp.dma_start(wraw[:, j, :], shared_w[n + 2]).then_inc(wraw_in[j], 16)
            for j in range(2):
                sp.wait_ge(w_split, NBLK + j + 1)
                sp.dma_start(wraw[:, j, :], shared_w[NBLK + 2 + j]).then_inc(wraw_in[j], 16)
            for j in range(2):
                sp.wait_ge(x1t_out[j], 16 * NBLK // 2 + 16)
                sp.wait_ge(x1_out[j], 16 * NBLK // 2 + 16)
            sp.wait_ge(tok_done, 4 * NBLK + 5)
            sp.dma_start(eraw[:, 0, 1], expert_w[0]).then_inc(er_in[0], 16)

            def load_res(n):
                sp.wait_ge(o_done, 4 * n)
                sp.dma_start(xres[:, :, :], x1_d[bass.ds(n * BLK, BLK), :].rearrange("(s p) d -> p s d", p=P)).then_inc(xres_in, 16)

            def store_out(n):
                sp.wait_ge(o_done, 4 * n + 4)
                sp.dma_start(out[bass.ds(n * BLK, BLK), :].rearrange("(s p) d -> p s d", p=P), outst[:, :, :]).then_inc(out_stored, 16)

            def load_x1t(n, j):
                sp.wait_ge(xh_ready, 4 * (NBLK + n + 1))
                sp.wait_ge(xl_ready, 4 * (NBLK + n + 1))
                sp.dma_start(xin[:, j], x1t_d[bass.ds(n + 2, 1)].rearrange("a p c t -> p (a c) t")).then_inc(xin_in[j], 16)

            load_x1t(0, 0)
            load_res(0)
            load_x1t(1, 1)
            store_out(0)
            load_res(1)

            def move_piece(n, hc, more=True):
                q = HC * (n - EBLK) + hc
                j = hc % 2
                if more:
                    sp.wait_ge(ehl_out[1 - j], 16 * (HC // 2 * (n - EBLK) + (hc + 1) // 2) + 16)
                    sp.dma_start(eraw[:, 1 - j, 1], expert_w[bass.ds(q + 1, 1)].rearrange("a p n -> p (a n)")).then_inc(er_in[1 - j], 16)
                sp.wait_ge(el_ready, q + 1)
                sp.dma_start(we_d[bass.ds(q, 1)].rearrange("a p s n -> p (a s) n").bitcast(FP32),
                             ehl[:, j].bitcast(FP32)).then_inc(ehl_out[j], 16)

            def middle_block(n, j, last=False):
                for hc in range(HC):
                    move_piece(n, hc, not (last and hc == HC - 1))
                    if hc == 1:
                        store_out(n - 1)
                        load_res(n)
                    if hc == 5:
                        load_x1t(n, j)

            with sp.Fori(EBLK // 2, NBLK // 2 - 2) as h:
                for j in range(2):
                    middle_block(2 * h + j, j)
            middle_block(NBLK - 4, 0)
            middle_block(NBLK - 3, 1, True)

            def load_weight(i):
                sp.dma_start(we[:, i // 2 % WRING, i % 2].rearrange("p h s c n -> p h s (c n)").bitcast(FP32),
                             we_d[2 * i:2 * i + 2].rearrange("h p s n -> p h s n").bitcast(FP32)).then_inc(we_in[i % HRING], 16)

            def weight_loaded(i):
                sp.wait_ge(we_in[i % HRING], 16 * (i // HRING) + 16)
                sp.sem_inc(weights_in, 1)

            for j in range(2):
                sp.wait_ge(ehl_out[j], 16 * EP // 2 + 16)
            load_weight(0)
            for n in (NBLK - 2, NBLK - 1):
                store_out(n - 1)
                load_res(n)
            weight_loaded(0)
            sp.wait_ge(ab_done, HC * NBLK)
            for i in range(1, 5):
                load_weight(i)
            store_out(NBLK - 1)
            for i in range(5, HRING):
                load_weight(i)
            for i in range(1, HRING):
                weight_loaded(i)
            for e in range(WRING, E):
                sp.wait_ge(mm2_done, sp.value_load(ends[0:1, e - WRING:e - WRING + 1], min_val=0, max_val=TILES) + 1)
                load_weight(2 * e)
                load_weight(2 * e + 1)
                weight_loaded(2 * e)
                weight_loaded(2 * e + 1)
            sp.wait_ge(pads_in, 48)
            sp.wait_ge(out_stored, 16 * NBLK)
            sp.wait_ge(added, 16 * TILES)

        @block.tensor
        def _(pe):
            pe.sem_inc(lin_done, 1)
            pe.sem_inc(tok_done, 5)
            pe.sem_inc(mm2_done, 1)
            pe.wait_ge(prep, 4)
            pe.wait_ge(small_in, 64)
            for o in range(DC):
                for c in range(DC):
                    pe.matmul(misc_ps[:, o * BATCH:(o + 1) * BATCH], w0sq[:, c, o * P:(o + 1) * P], modsq[:, c, :],
                              start=(c == 0), stop=(c == DC - 1))
            for b in range(BATCH):
                for c in range(DC):
                    last = pe.matmul(misc_ps[:, 16 + b * E:16 + (b + 1) * E], condb[:, c, b, :], rw[:, DC + c, :],
                                     start=(c == 0), stop=(c == DC - 1))
            last.then_inc(misc_done, 1)

            def linear(n, wb, j):
                for o in range(DC):
                    pe.wait_ge(x1t_done, 4 * n + o + 1)
                    for c in range(DC):
                        if o == 0:
                            pe.wait_ge(xl_ready, 4 * n + c + 1)
                        w_hi, w_lo = wmh[:, wb, c, o * P:(o + 1) * P], wml[:, wb, c, o * P:(o + 1) * P]
                        pe.matmul(lin_ps[o % 2][:, :], w_hi, xh[:, j, c, :], start=(c == 0), stop=False)
                        pe.matmul(lin_ps[o % 2][:, :], w_hi, xl[:, j, c, :], start=False, stop=False)
                        last = pe.matmul(lin_ps[o % 2][:, :], w_lo, xh[:, j, c, :], start=False, stop=(c == DC - 1))
                    last.then_inc(lin_done, 1)

            def by_token(n, j):
                pe.wait_ge(x1t_done, 4 * n + DC + 2)
                for s in range(SUB):
                    pe.wait_ge(x1_done, 4 * n + s + 1)
                    for o in range(DC):
                        pe.matmul(logit_ps[:, bass.ds((n * SUB + s) * E, E)], x1t[:, j, o, s * P:(s + 1) * P], rw[:, o, :],
                                  start=(o == 0), stop=(o == DC - 1))
                    for o in range(DC):
                        last = pe.transpose(tok_ps[s % 2][:, o * P:(o + 1) * P], x1t[:, j, o, s * P:(s + 1) * P], ident)
                    last.then_inc(tok_done, 1)

            with pe.Fori(0, NBLK // 4) as i:
                for k in range(4):
                    if k % 2 == 0:
                        pe.wait_ge(wml_ready, DC * (2 * i + k // 2 + 1))
                    linear(4 * i + k, k // 2, k % 2)
                    if k:
                        by_token(4 * i + k - 1, (k - 1) % 2)
                by_token(4 * i + 3, 1)

            def up(n, hc, j):
                q = HC * n + hc
                if hc == 0:
                    pe.wait_ge(xl_ready, 4 * (NBLK + n + 1))
                pe.wait_ge(gm_done, q + 1)
                for ps, m in ((a_ps, 0), (b_ps, 1)):
                    for c in range(DC):
                        w_hi, w_lo = w13h[:, hc, m, c, :], w13l[:, hc, m, c, :]
                        pe.matmul(ps[hc % 2][:, :], w_hi, xh[:, j, c, :], start=(c == 0), stop=False)
                        pe.matmul(ps[hc % 2][:, :], w_hi, xl[:, j, c, :], start=False, stop=False)
                        last = pe.matmul(ps[hc % 2][:, :], w_lo, xh[:, j, c, :], start=False, stop=(c == DC - 1))
                last.then_inc(ab_done, 1)

            def down(n, hc):
                q = HC * n + hc
                pe.wait_ge(gl_ready, q + 1)
                if hc == 0:
                    pe.wait_ge(o_done, 4 * n)
                k = hc % 2
                for s in range(SUB):
                    g_hi, g_lo = gh[:, k, s * P:(s + 1) * P], gl[:, k, s * P:(s + 1) * P]
                    pe.matmul(o_ps[s][:, :], g_hi, w2h[:, hc, :], start=(hc == 0), stop=False)
                    pe.matmul(o_ps[s][:, :], g_hi, w2l[:, hc, :], start=False, stop=False)
                    last = pe.matmul(o_ps[s][:, :], g_lo, w2h[:, hc, :], start=False, stop=(hc == HC - 1))
                last.then_inc(down_done, 1)

            def shared_block(n, j):
                for hc in range(HC):
                    up(n, hc, j)
                    if hc:
                        down(n, hc - 1)
                    else:
                        down(n - 1, HC - 1)

            pe.wait_ge(w_split, HC)
            pe.wait_ge(x1t_done, DC * NBLK + 2)
            pe.wait_ge(x1_done, SUB * NBLK + 2)
            up(0, 0, 0)
            pe.wait_ge(logit_done, 1)
            for hc in range(1, HC):
                up(0, hc, 0)
                pe.wait_ge(w_split, HC + 1 + (hc - 1) // 2)
                down(0, hc - 1)
            for hc in range(HC):
                up(1, hc, 1)
                if hc:
                    down(1, hc - 1)
                else:
                    down(0, HC - 1)
                if hc == 5:
                    pe.wait_ge(mask_done, 1)
                    pe.wait_ge(gm_done, HC + hc - 1 + 1 + 2)
                    pe.matmul(rank_ps[:, 0:NT * E], tri, rt[:, 4, :], start=True, stop=True)
                    pe.matmul(rank_ps[:, NT * E:2 * NT * E], ones, rt[:, 4, :], start=True, stop=True).then_inc(rank_mm, 1)
                    pe.wait_ge(rank_done, 1)
            with pe.Fori(1, NBLK // 2) as h:
                for j in range(2):
                    shared_block(2 * h + j, j)

            def transpose_x(t, k, turn):
                if k % PAIR == 0:
                    pe.wait_ge(xg_in[k // PAIR % 2], 16 * turn + 16)
                pe.wait_ge(xgt_done, t + 1)
                for c in range(DC):
                    last = pe.transpose(xt_ps[k % 2][:, c * P:(c + 1) * P], xg[:, k % RING, c * P:(c + 1) * P], ident)
                last.then_inc(tx_done, 1)

            def transpose_h(t, k):
                pe.wait_ge(hid_done, t + 1 + 2)
                pe.wait_ge(hidt_done, t + 1)
                for c in range(DC):
                    last = pe.transpose(ht_ps[k % 2][:, c * P:(c + 1) * P], hid[:, k % 2, c * P:(c + 1) * P], ident)
                last.then_inc(th_done, 1)

            def product(ps, high, low, place, m):
                for c in range(DC):
                    w_hi, w_lo = (we[:, bass.ds(place, 1), m, c // 2, part, c % 2, :].rearrange("p a n -> p (a n)") for part in range(2))
                    pe.matmul(ps, high[:, c, :], w_hi, start=(c == 0), stop=False)
                    pe.matmul(ps, high[:, c, :], w_lo, start=False, stop=False)
                    last = pe.matmul(ps, low[:, c, :], w_hi, start=False, stop=(c == DC - 1))
                return last

            def expert_of(t):
                return (pe.value_load(etab[0:1, bass.ds(t, 1)], min_val=0, max_val=E - 1),
                        pe.value_load(eplace[0:1, bass.ds(t, 1)], min_val=0, max_val=WRING - 1))

            def matmul1(t, k):
                e, place = expert_of(t)
                pe.wait_ge(weights_in, 2 * e + 1)
                pe.wait_ge(xgt_done, t + 1 + 2)
                pe.wait_ge(hid_done, t + 1)
                product(h_ps[k % 2][:, :], xgth[:, k % 2], xgtl[:, k % 2], place, 0).then_inc(mm1_done, 1)

            def matmul2(t, k):
                e, place = expert_of(t)
                pe.wait_ge(weights_in, 2 * e + 2)
                pe.wait_ge(hidt_done, t + 1 + 2)
                pe.wait_ge(ys_done, t + 1)
                product(y_ps[k % 2][:, :], hidth[:, k % 2], hidtl[:, k % 2], place, 1).then_inc(mm2_done, 1)

            pe.wait_ge(etab_done, 3)
            pe.wait_ge(gm_done, HC * NBLK - 1 + 2)
            transpose_x(0, 0, 0)
            down(NBLK - 1, HC - 1)
            pe.wait_ge(gm_done, HC * NBLK + 2)
            matmul1(0, 0)
            transpose_x(1, 1, 0)
            pe.wait_ge(o_done, SUB * NBLK)
            transpose_h(0, 0)
            with pe.Fori(0, TILES // RING - 1) as i:
                for k in range(1, RING + 1):
                    t = RING * i + k
                    matmul1(t, k)
                    transpose_x(t + 1, k + 1, i + (k + 1) // RING)
                    matmul2(t - 1, k - 1)
                    transpose_h(t, k)
            for t in range(TILES - RING + 1, TILES):
                matmul1(t, t)
                if t + 1 < TILES:
                    transpose_x(t + 1, t + 1, (t + 1) // RING)
                matmul2(t - 1, t - 1)
                transpose_h(t, t)
            matmul2(TILES - 1, TILES - 1)

        @block.scalar
        def _(act):
            act.sem_inc(x1_done, 2)
            act.sem_inc(hid_done, 2)
            act.wait_ge(prep, 5)
            act.activation(dtmp[:, :, :], dvar[:, :, :], ACT.Sqrt).then_inc(root, 1)

            def x_high(j, c):
                act.activation(xh[:, j, c, :], xin[:, j, c, :], ACT.Copy).then_inc(xh_ready, 1)

            def weight_high(b, wb, i):
                act.wait_ge(lin_done, 4 * DC * i + 1)
                for c in range(DC):
                    act.activation(wmh[:, wb, c, :], w0s[:, c, :], ACT.Copy,
                                   scale=mod[:, c, bass.ds(b, 1)]).then_inc(wmh_ready, 1)

            def by_token(n, turn, j):
                act.wait_ge(x1_out[j], 16 * turn + 16)
                for s in range(SUB):
                    act.wait_ge(tok_done, 4 * n + s + 1 + 5)
                    act.activation(x1tok[:, j, s, :], tok_ps[s % 2][:, :], ACT.Copy).then_inc(x1_done, 1)
                act.wait_ge(x1_done, SUB * n + SUB + 2)
                act.dma_start(x1_d[bass.ds(n * BLK, BLK), :].rearrange("(s p) d -> p s d", p=P), x1tok[:, j]).then_inc(x1_out[j], 16)

            act.wait_ge(xin_in[0], 16)
            for c in range(DC):
                x_high(0, c)
            with act.Fori(0, NBLK // 4) as i:
                weight_high(2 * i, 0, i)
                for k in range(4):
                    n = 4 * i + k
                    act.wait_ge(xin_in[(k + 1) % 2], 16 * (2 * i + (k + 1) // 2) + 16)
                    act.wait_ge(lin_done, DC * n + 1)
                    for c in range(DC):
                        x_high((k + 1) % 2, c)
                    if k == 0:
                        weight_high(2 * i + 1, 1, i)
                    act.wait_ge(wraw_in[k % 2], 16 * (2 * i + k // 2) + 16)
                    act.activation(w13h[:, bass.ds(n, 1)].rearrange("p a m c n -> p (a m c n)"), wraw[:, k % 2, :],
                                   ACT.Copy).then_inc(w_high, 1)
                    if k:
                        by_token(n - 1, 2 * i + (k - 1) // 2, (k - 1) % 2)
                by_token(4 * i + 3, 2 * i + 1, 1)

            def w2_high(g):
                act.wait_ge(wraw_in[g % 2], 16 * ((HC + g) // 2) + 16)
                act.wait_ge(lin_done, DC * NBLK + 1)
                act.activation(w2h[:, 2 * g:2 * g + 2, :].rearrange("p b n -> p (b n)"), wraw[:, g % 2, :],
                               ACT.Copy).then_inc(w_high, 1)

            w2_high(0)
            act.wait_ge(logit_done, 1)
            act.activation(score[:, :, :], score[:, :, :], ACT.Sigmoid).then_inc(score_done, 1)

            def gate(n, hc):
                act.wait_ge(ab_done, HC * n + hc + 1)
                act.activation(sil[:, hc % 2, :], a_ps[hc % 2][:, :], ACT.Silu).then_inc(sil_done, 1)

            def hidden_high(n, hc):
                act.wait_ge(gm_done, HC * n + hc + 1 + 2)
                act.activation(gh[:, hc % 2, :], gm[:, hc % 2, :], ACT.Copy).then_inc(gh_ready, 1)

            def next_high(n, hc, j, turn):
                if hc == 2:
                    act.wait_ge(xin_in[(j + 1) % 2], 16 * turn + 16)
                    act.wait_ge(ab_done, HC * n)
                if 2 <= hc < 2 + DC:
                    x_high((j + 1) % 2, hc - 2)

            def block_steps(n, j, turn):
                for hc in range(HC):
                    gate(n, hc)
                    if turn is not None:
                        next_high(n, hc, j, turn)
                    hidden_high(n, hc)

            for hc in range(HC):
                gate(0, hc)
                next_high(0, hc, 0, NBLK // 2)
                hidden_high(0, hc)
                if hc in (0, 2, 4):
                    w2_high(1 + hc // 2)
            block_steps(1, 1, NBLK // 2 + 1)

            def middle_steps(n, j, turn):
                for hc in range(HC):
                    gate(n, hc)
                    next_high(n, hc, j, turn)
                    hidden_high(n, hc)
                    act.wait_ge(er_in[hc % 2], 16 * (HC // 2 * (n - EBLK) + hc // 2) + 16)
                    act.activation(ehl[:, hc % 2, 0], eraw[:, hc % 2, 1], ACT.Copy).then_inc(eh_ready, 1)

            with act.Fori(1, NBLK // 2 - 1) as h:
                middle_steps(2 * h, 0, NBLK // 2 + h)
                middle_steps(2 * h + 1, 1, NBLK // 2 + h + 1)
            block_steps(NBLK - 2, 0, NBLK - 1)

            def load_rows(t, k, turn):
                j = k // PAIR % 2
                act.wait_ge(staged[j], 16 * turn + 16)
                act.dma_start(xg[:, k % RING:k % RING + PAIR, :],
                              xs_d[bass.ds(t * P, PAIR * P), :].rearrange("(t p) d -> p t d", p=P)).then_inc(xg_in[j], 16)

            act.wait_ge(xl_ready, DC * 2 * NBLK)
            load_rows(0, 0, 0)
            load_rows(PAIR, PAIR, 0)
            block_steps(NBLK - 1, 1, None)

            def take_x(t, k):
                act.wait_ge(tx_done, t + 1)
                act.activation(xgth[:, k % 2].rearrange("p c n -> p (c n)"), xt_ps[k % 2][:, :], ACT.Copy).then_inc(xgth_done, 1)

            def experts_step(t, k, turn, more=True, rows=True):
                act.wait_ge(mm1_done, t + 1)
                act.activation(hid[:, k % 2, :], h_ps[k % 2][:, :], ACT.Gelu).then_inc(hid_done, 1)
                if more:
                    take_x(t + 1, k + 1)
                    if k % PAIR == 0 and rows:
                        load_rows(t + RING, k, turn + 1)
                act.wait_ge(th_done, t + 1)
                act.activation(hidth[:, k % 2].rearrange("p c n -> p (c n)"), ht_ps[k % 2][:, :], ACT.Copy).then_inc(hidth_done, 1)

            take_x(0, 0)
            with act.Fori(0, TILES // RING - 1) as i:
                for k in range(RING):
                    experts_step(RING * i + k, k, i)
            for t in range(TILES - RING, TILES):
                experts_step(t, t, 0, t + 1 < TILES, False)

        @block.vector
        def _(dve):
            steps = [0]

            def then(ins):
                steps[0] += 1
                ins.then_inc(step, 1)
                dve.wait_ge(step, steps[0])

            dve.sem_inc(x1t_done, 2)
            dve.sem_inc(gm_done, 2)
            dve.sem_inc(xgt_done, 2)
            dve.sem_inc(hidt_done, 2)
            dve.sem_inc(ys_done, 2)
            dve.wait_ge(cond_in, 16)
            dve.tensor_scalar(mod[:, :, :], cnd[:, :, :], float(np.float32(1.0) / np.sqrt(np.float32(D))), None, ALU.mult).then_inc(prep, 1)
            dve.tensor_copy(condb[:, :, :, :], cnd[:, :, :].unsqueeze(3).to_broadcast([P, DC, BATCH, P])).then_inc(prep, 1)
            dve.wait_ge(prep, 2)
            dve.tensor_tensor(modsq[:, :, :], mod[:, :, :], mod[:, :, :], ALU.mult).then_inc(prep, 1)
            dve.wait_ge(w0_in, 16)
            dve.tensor_tensor(w0sq[:, :, :], w0s[:, :, :], w0s[:, :, :], ALU.mult).then_inc(prep, 1)
            dve.wait_ge(misc_done, 1)
            dve.tensor_scalar(dvar[:, :, :].rearrange("p c b -> p (c b)"), misc_ps[:, 0:DC * BATCH], EPS, None,
                              ALU.add).then_inc(prep, 1)
            dve.tensor_copy(rconst[:, :, :].rearrange("p b e -> p (b e)"), misc_ps[:, 16:16 + BATCH * E])
            dve.wait_ge(root, 1)
            then(dve.reciprocal(dsc[:, :, :], dtmp[:, :, :]))
            then(dve.tensor_tensor(dtmp[:, :, :], dsc[:, :, :], dsc[:, :, :], ALU.mult))
            then(dve.tensor_tensor(dtmp[:, :, :], dtmp[:, :, :], dvar[:, :, :], ALU.mult))
            then(dve.tensor_scalar(dtmp[:, :, :], dtmp[:, :, :], -0.5, 1.5, ALU.mult, ALU.add))
            then(dve.tensor_tensor(dsc[:, :, :], dsc[:, :, :], dtmp[:, :, :], ALU.mult))

            def x_low(m, j, c):
                dve.wait_ge(xh_ready, DC * m + c + 1)
                dve.tensor_tensor(xl[:, j, c, :], xin[:, j, c, :], xh[:, j, c, :].bitcast(FP32), ALU.subtract).then_inc(xl_ready, 1)

            def weight_low(b, wb):
                for c in range(DC):
                    dve.wait_ge(wmh_ready, DC * b + c + 1)
                    dve.scalar_tensor_tensor(wml[:, wb, c, :], w0s[:, c, :], mod[:, c, bass.ds(b, 1)],
                                             wmh[:, wb, c, :].bitcast(FP32), ALU.mult, ALU.subtract).then_inc(wml_ready, 1)

            for c in range(DC):
                x_low(0, 0, c)
            with dve.Fori(0, NBLK // 4) as i:
                weight_low(2 * i, 0)
                for k in range(4):
                    n, j = 4 * i + k, k % 2
                    for o in range(DC):
                        dve.wait_ge(lin_done, DC * n + o + 1 + 1)
                        if o == 0:
                            dve.wait_ge(x1t_out[j], 16 * (2 * i + k // 2) + 16)
                            dve.wait_ge(tok_done, 4 * n - 4 + 5)
                        dve.scalar_tensor_tensor(x1t[:, j, o, :], lin_ps[o % 2][:, :], dsc[:, o, bass.ds(2 * i + k // 2, 1)],
                                                 xin[:, j, o, :], ALU.mult, ALU.add).then_inc(x1t_done, 1)
                        x_low(n + 1, (k + 1) % 2, o)
                    if k == 0:
                        weight_low(2 * i + 1, 1)
                    dve.wait_ge(w_high, n + 1)
                    w_hi = w13h[:, bass.ds(n, 1)].rearrange("p a m c n -> p (a m c n)").bitcast(FP32)
                    dve.tensor_tensor(w13l[:, bass.ds(n, 1)].rearrange("p a m c n -> p (a m c n)"), wraw[:, j, :],
                                      w_hi, ALU.subtract).then_inc(w_split, 1)

            def w2_low(g):
                dve.wait_ge(w_high, HC + g + 1)
                dve.tensor_tensor(w2l[:, 2 * g:2 * g + 2, :].rearrange("p b n -> p (b n)"), wraw[:, g % 2, :],
                                  w2h[:, 2 * g:2 * g + 2, :].rearrange("p b n -> p (b n)").bitcast(FP32),
                                  ALU.subtract).then_inc(w_split, 1)

            w2_low(0)
            dve.wait_ge(tok_done, 4 * NBLK + 5)
            dve.tensor_tensor(score[:, :, :].rearrange("p (b t) e -> p b t e", b=BATCH),
                              logit_ps[:, 0:NT * E].rearrange("p (b t e) -> p b t e", b=BATCH, e=E),
                              rconst[:, :, :].unsqueeze(2).to_broadcast([P, BATCH, NT // BATCH, E]), ALU.add).then_inc(logit_done, 1)

            def product(n, hc):
                dve.wait_ge(sil_done, HC * n + hc + 1)
                dve.tensor_tensor(gm[:, hc % 2, :], sil[:, hc % 2, :], b_ps[hc % 2][:, :], ALU.mult).then_inc(gm_done, 1)

            def hidden_low(n, hc):
                dve.wait_ge(gh_ready, HC * n + hc + 1)
                dve.tensor_tensor(gl[:, hc % 2, :], gm[:, hc % 2, :], gh[:, hc % 2, :].bitcast(FP32), ALU.subtract).then_inc(gl_ready, 1)

            def output(n):
                dve.wait_ge(down_done, HC * (n + 1))
                dve.wait_ge(xres_in, 16 * (n + 1))
                dve.wait_ge(out_stored, 16 * n)
                for s in range(SUB):
                    dve.scalar_tensor_tensor(outst[:, s, :], o_ps[s][:, :], THIRD, xres[:, s, :], ALU.mult, ALU.add).then_inc(o_done, 1)

            def block_step(n, hc, j, more):
                product(n, hc)
                if more and 2 <= hc < 2 + DC:
                    x_low(NBLK + n + 1, (j + 1) % 2, hc - 2)
                hidden_low(n, hc)

            def row(r, shape=(NT, E), dt=None):
                v = rt[:, r, :] if dt is None else rt[:, r, :].bitcast(dt)
                return v.rearrange("p (a b) -> p a b", b=shape[1])

            def per_tile(v):
                return v.unsqueeze(2).to_broadcast([P, NT, E])

            def per_expert(v):
                return v.unsqueeze(1).to_broadcast([P, NT, E])

            SEL, KEY, CHOICE, MASK = 0, 1, (2, 3), 4
            rev = cst[:, C_REV:C_REV + E]

            def choose(k):
                then(dve.tensor_reduce(s32[:, 0, :], row(SEL), AX.X, ALU.max))
                then(dve.tensor_tensor(row(KEY), row(SEL), per_tile(s32[:, 0, :]), ALU.is_equal))
                then(dve.tensor_tensor(row(KEY), row(KEY), per_expert(rev), ALU.mult))
                then(dve.tensor_reduce(s32[:, 0, :], row(KEY), AX.X, ALU.max))
                then(dve.tensor_tensor(row(CHOICE[k]), row(KEY), per_tile(s32[:, 0, :]), ALU.is_equal))
                then(dve.tensor_tensor(row(KEY), score[:, :, :], row(CHOICE[k]), ALU.mult))
                then(dve.tensor_reduce(s32[:, 1 + k, :], row(KEY), AX.X, ALU.add))
                if k == 0:
                    then(dve.scalar_tensor_tensor(row(SEL), row(CHOICE[0]), -3.0e38, row(SEL), ALU.mult, ALU.add))

            def gates():
                then(dve.tensor_tensor(s32[:, 3, :], s32[:, 1, :], s32[:, 2, :], ALU.add))
                then(dve.tensor_scalar(s32[:, 4, :], s32[:, 3, :], 1e-9, None, ALU.add))
                then(dve.reciprocal(s32[:, 5, :], s32[:, 4, :]))
                then(dve.tensor_scalar(s32[:, 6, :], s32[:, 3, :], 1e-9, None, ALU.is_gt))
                then(dve.tensor_scalar(s32[:, 7, :], s32[:, 6, :], -1.0 / K, 1.0 / K, ALU.mult, ALU.add))
                then(dve.tensor_tensor(s32[:, 5, :], s32[:, 5, :], s32[:, 6, :], ALU.mult))
                for k in range(K):
                    then(dve.tensor_tensor(s32[:, 1 + k, :], s32[:, 1 + k, :], s32[:, 5, :], ALU.mult))
                    then(dve.tensor_tensor(s32[:, 1 + k, :], s32[:, 1 + k, :], s32[:, 7, :], ALU.add))
                    then(dve.tensor_scalar(rec[:, k, :, 1].bitcast(FP32), s32[:, 1 + k, :], THIRD, None, ALU.mult))
                    then(dve.tensor_copy(rec[:, k, :, 0], tid[:, :]))

            WITHIN, TOTAL, PING, PONG, POS = 0, 1, 5, 6, 7

            def scan_tiles():
                src = TOTAL
                for d, dst in ((1, PING), (2, PONG), (4, PING), (8, PONG), (16, PING)):
                    dve.tensor_copy(row(dst)[:, 0:d, :], row(src)[:, 0:d, :])
                    then(dve.tensor_tensor(row(dst)[:, d:NT, :], row(src)[:, d:NT, :], row(src)[:, 0:NT - d, :], ALU.add))
                    src = dst

            def first_slots():
                count = row(PING)[:, NT - 1, :]
                then(dve.tensor_tensor(row(PONG, (E, NT)), count.unsqueeze(2).to_broadcast([P, E, NT]),
                                       cst[:, C_THR:C_THR + NT].unsqueeze(1).to_broadcast([P, E, NT]), ALU.is_gt))
                then(dve.tensor_reduce(e8[:, 0, :], row(PONG, (E, NT)), AX.X, ALU.add))
                src = 0
                for d, dst in ((1, 1), (2, 2), (4, 1)):
                    dve.tensor_copy(e8[:, dst, 0:d], e8[:, src, 0:d])
                    then(dve.tensor_tensor(e8[:, dst, d:E], e8[:, src, d:E], e8[:, src, 0:E - d], ALU.add))
                    src = dst
                then(dve.tensor_tensor(e8[:, 3, :], e8[:, 1, :], e8[:, 0, :], ALU.subtract))
                then(dve.tensor_scalar(e8[:, 4, :], e8[:, 3, :], float(P), None, ALU.mult))
                then(dve.tensor_tensor(row(POS), row(PING), row(TOTAL), ALU.subtract))
                then(dve.tensor_tensor(row(POS), row(POS), row(WITHIN), ALU.add))
                then(dve.tensor_tensor(row(POS), row(POS), per_expert(e8[:, 4, :]), ALU.add))

            def slot_rows():
                for k in range(K):
                    pos = s32[:, 3, :].bitcast(INT32)
                    tile_, part = s32[:, 4, :].bitcast(INT32), s32[:, 5, :].bitcast(INT32)
                    then(dve.tensor_tensor(row(PONG), row(CHOICE[k]), row(POS), ALU.mult))
                    then(dve.tensor_reduce(s32[:, 0, :], row(PONG), AX.X, ALU.add))
                    then(dve.tensor_copy(pos, s32[:, 0, :]))
                    then(dve.tensor_single_scalar(tile_, pos, 7, ALU.logical_shift_right))
                    then(dve.tensor_single_scalar(part, pos, P - 1, ALU.bitwise_and))
                    dve.scalar_tensor_tensor(sadr[:, k, :], part, float(TILES), tile_, ALU.mult, ALU.add).then_inc(sadr_done, 1)

            def expert_table():
                cmp_ = rt[0:1, PING:PING + 3, :].rearrange("p a b -> p (a b)")[:, 0:TILES * E].rearrange("p (t e) -> p t e", e=E)
                then(dve.tensor_tensor(cmp_, e8[0:1, 1, :].unsqueeze(1).to_broadcast([1, TILES, E]),
                                       cst[0:1, C_TIX:C_TIX + TILES].unsqueeze(2).to_broadcast([1, TILES, E]), ALU.is_le))
                etf = rt[0:1, WITHIN, 0:TILES]
                then(dve.tensor_reduce(etf, cmp_, AX.X, ALU.add))
                then(dve.tensor_scalar(etf, etf, float(E - 1), None, ALU.min))
                dve.tensor_copy(etab[0:1, :], etf).then_inc(etab_done, 1)
                place = rt[0:1, TOTAL, 0:TILES]
                then(dve.tensor_scalar(place, etf, float(WRING), float(-WRING), ALU.is_ge, ALU.mult))
                dve.tensor_tensor(eplace[0:1, :], place, etf, ALU.add).then_inc(etab_done, 1)
                dve.tensor_copy(ends[:, :], e8[:, 1, :]).then_inc(etab_done, 1)

            for hc in range(HC):
                block_step(0, hc, 0, True)
                if hc in (0, 2, 4):
                    w2_low(1 + hc // 2)
                if hc == 5:
                    dve.wait_ge(score_done, 1)
                    then(dve.tensor_tensor(row(SEL), score[:, :, :], per_expert(rb[:, :]), ALU.add))
                if hc == 6:
                    choose(0)
                if hc == 7:
                    choose(1)
            for hc in range(HC):
                block_step(1, hc, 1, True)
                if hc == 0:
                    output(0)
                if hc == 1:
                    dve.tensor_tensor(row(MASK), row(CHOICE[0]), row(CHOICE[1]), ALU.add).then_inc(mask_done, 1)
                    gates()
                if hc == 5:
                    dve.wait_ge(rank_mm, 1)
                    then(dve.tensor_copy(rt[:, WITHIN:TOTAL + 1, :].rearrange("p a b -> p (a b)"), rank_ps[:, :]))
                    dve.sem_inc(rank_done, 1)
                    scan_tiles()
                if hc == 6:
                    first_slots()
                if hc == 7:
                    slot_rows()
                    expert_table()

            def piece_low(n, hc):
                dve.wait_ge(eh_ready, HC * (n - EBLK) + hc + 1)
                dve.tensor_tensor(ehl[:, hc % 2, 1], eraw[:, hc % 2, 1], ehl[:, hc % 2, 0].bitcast(FP32), ALU.subtract).then_inc(el_ready, 1)

            with dve.Fori(1, NBLK // 2 - 1) as h:
                for j in range(2):
                    for hc in range(HC):
                        block_step(2 * h + j, hc, j, True)
                        if hc == 0:
                            output(2 * h + j - 1)
                        piece_low(2 * h + j, hc)
            for n in (NBLK - 2, NBLK - 1):
                for hc in range(HC):
                    block_step(n, hc, n % 2, n < NBLK - 1)
                    if hc == 0:
                        output(n - 1)
            output(NBLK - 1)

            def take_x(t, k):
                dve.wait_ge(xgth_done, t + 1)
                dve.tensor_tensor(xgtl[:, k % 2].rearrange("p c n -> p (c n)"), xt_ps[k % 2][:, :],
                                  xgth[:, k % 2].rearrange("p c n -> p (c n)").bitcast(FP32), ALU.subtract).then_inc(xgt_done, 1)

            def take_h(t, k):
                dve.wait_ge(hidth_done, t + 1)
                dve.tensor_tensor(hidtl[:, k % 2].rearrange("p c n -> p (c n)"), ht_ps[k % 2][:, :],
                                  hidth[:, k % 2].rearrange("p c n -> p (c n)").bitcast(FP32), ALU.subtract).then_inc(hidt_done, 1)

            def take_y(t, k, reused=True):
                dve.wait_ge(mm2_done, t + 1 + 1)
                if reused:
                    dve.wait_ge(added, 16 * (t + 1 - RING))
                dve.tensor_scalar(ys[:, k % RING, :], y_ps[k % 2][:, :], slot[:, bass.ds(t, 1), 1].bitcast(FP32), None,
                                  ALU.mult).then_inc(ys_done, 1)

            dve.wait_ge(slots_in, 16)
            take_x(0, 0)
            take_x(1, 1)
            take_h(0, 0)
            for t in range(1, RING + 1):
                take_x(t + 1, t + 1)
                take_y(t - 1, t - 1, False)
                take_h(t, t)
            with dve.Fori(1, TILES // RING - 1) as i:
                for k in range(1, RING + 1):
                    t = RING * i + k
                    take_x(t + 1, k + 1)
                    take_y(t - 1, k - 1)
                    take_h(t, k)
            for t in range(TILES - RING + 1, TILES):
                if t + 1 < TILES:
                    take_x(t + 1, t + 1)
                take_y(t - 1, t - 1)
                take_h(t, t)
            take_y(TILES - 1, TILES - 1)

        @block.gpsimd
        def _(pool):
            IO = bass.IndirectOffsetOnAxis
            pool.wait_ge(pads_in, 48)
            for k in range(K):
                pool.wait_ge(sadr_done, k + 1)
                for i in range(NT):
                    pool.indirect_dma_start(slots_d[:, :], IO(sadr[:, k, i:i + 1], 0), rec[:, k, i, :], None).then_inc(listed, 16)

            pool.wait_ge(listed, 16 * K * NT)
            pool.dma_start(slot[:, :, :], slots_d[:, :].rearrange("(p t) c -> p t c", p=P)).then_inc(slots_in, 16)
            pool.wait_ge(slots_in, 16)
            pool.wait_ge(etab_done, 3)
            for j in range(2):
                pool.wait_ge(x1_out[j], 16 * NBLK // 2 + 16)

            def store_rows(g):
                pool.wait_ge(rows_in[g % 2], 16 * PAIR * (g // 2 + 1))
                pool.dma_start(xs_d[g * PAIR * P:(g + 1) * PAIR * P, :].rearrange("(t p) d -> p t d", p=P),
                               xs[:, g % 2]).then_inc(staged[g % 2], 16)

            for g in range(TILES // PAIR):
                if g >= 2:
                    pool.wait_ge(staged[g % 2], 16 * (g // 2))
                for k in range(PAIR):
                    t = g * PAIR + k
                    pool.indirect_dma_start(xs[:, g % 2, k, :], None, x1_d[:, :], IO(slot[:, t, 0:1], 0)).then_inc(rows_in[g % 2], 16)
                if g:
                    store_rows(g - 1)
            store_rows(TILES // PAIR - 1)

            def scatter(t, k, copies):
                if not isinstance(t, int) or t:
                    pool.wait_ge(added, 16 * t)
                pool.tensor_copy(six[k][:, :], slot[:, bass.ds(t, 1), 0]).then_inc(ixc, 1)
                pool.wait_ge(ys_done, t + 1 + 2)
                pool.wait_ge(ixc, copies)
                pool.sem_inc(issue, 1)
                pool.indirect_dma_start(out[:, :], IO(six[k][:, :], 0), ys[:, k, :], None,
                                        compute_op=ALU.add).then_inc(added, 16)

            pool.wait_ge(out_stored, 16 * NBLK)
            for t in range(RING):
                scatter(t, t, t + 1)
            with pool.Fori(1, TILES // RING) as i:
                for k in range(RING):
                    scatter(RING * i + k, k, RING * i + k + 1)


def _by_partition(a, chunks):
    a = a.reshape(*a.shape[:-2], chunks, P, a.shape[-1])
    return np.ascontiguousarray(np.swapaxes(a, -3, -2))


def _constants():
    c = np.zeros((P, C_END), np.float32)
    c[:, C_ID:C_ID + P] = np.eye(P)
    c[:, C_TRI:C_TRI + P] = np.triu(np.ones((P, P)), 1)
    c[:, C_ONE:C_ONE + P] = 1.0
    c[:, C_THR:C_THR + NT] = P * np.arange(NT)
    c[:, C_REV:C_REV + E] = E - np.arange(E)
    c[:, C_TIX:C_TIX + TILES] = np.arange(TILES)
    tokid = (P * np.arange(NT)[None, :] + np.arange(P)[:, None]).astype(np.int32)
    pads = np.zeros((P, TILES, 2), np.int32)
    pads[:, :, 0] = TOK + np.arange(P)[:, None]
    return c, tokid, pads.reshape(P, 2 * TILES)


def kernel(**inputs):
    import concourse.bacc as bacc
    from concourse.bass_utils import run_bass_kernel_spmd

    a = {k: np.asarray(v) for k, v in inputs.items()}
    xT = a["x"].reshape(NBLK, BLK, D).transpose(0, 2, 1)
    w13 = np.stack([a["L1_cond_w1"], a["L1_cond_w3"]]).reshape(2, DC, P, HC, P).transpose(3, 2, 0, 1, 4)
    w2 = a["L1_cond_w2"].reshape(HC // 2, 2, P, D).transpose(0, 2, 1, 3)
    experts = np.stack([_by_partition(a["L1_cond_W1e"], DC), _by_partition(a["L1_cond_W2e"], DC)], axis=1)
    experts = experts.reshape(2 * E, P, HALF // PIECE, PIECE).swapaxes(1, 2).reshape(EP, P, PIECE)
    consts, tokid, pads = _constants()
    arrays = {
        "xT": _by_partition(xT, DC),
        "w0": _by_partition(a["L0_cond_weight"], DC),
        "condT": _by_partition(a["cond_1024"].T, DC),
        "router_w": _by_partition(a["L1_cond_router_W"], 2 * DC),
        "router_b": np.ascontiguousarray(np.broadcast_to(a["L1_cond_router_bias"], (P, E))),
        "shared_w": np.concatenate([w13.reshape(HC, P, 1024), w2.reshape(HC // 2, P, 1024)]),
        "expert_w": np.ascontiguousarray(experts),
        "consts": consts,
        "tokid": tokid,
        "padslots": pads,
        "padrows": np.zeros((PADROWS, D), np.float32),
    }
    nc = bacc.Bacc("TRN2", target_bir_lowering=False, num_devices=1)
    args = {n: nc.dram_tensor(n, v.shape, mybir.dt.from_np(v.dtype), kind="ExternalInput").ap() for n, v in arrays.items()}
    out = nc.dram_tensor("out", (TOK + PADROWS, D), FP32, kind="ExternalOutput").ap()
    shared_moe_kernel(nc, **args, out=out)
    r = run_bass_kernel_spmd(nc, [arrays], core_ids=[0])
    return r.results[0]["out"][:TOK].reshape(BATCH, SEQ, D)
```

```python
import numpy as np

import concourse.bass as bass
from concourse import mybir
from concourse.alu_op_type import AluOpType as ALU
from contextlib import ExitStack

FP32 = mybir.dt.float32
FP32R = mybir.dt.float32r
INT32 = mybir.dt.int32
ACT = mybir.ActivationFunctionType
AX = mybir.AxisListType

P = 128
BATCH, SEQ, D = 4, 1024, 512
TOK = BATCH * SEQ
DC = D // P
HS = 1024
HC = HS // P
HE = 512
E = 8
K = 2
BLK = 512
NBLK = TOK // BLK
SUB = BLK // P
NT = TOK // P
RING = 4
TILES = K * TOK // P + E - 1
PAIR = 2
PADDED = -(-TILES // PAIR) * PAIR
SLOTS = PADDED * P
TURNS = TILES // RING
PADROWS = P
EPS = 1e-8
THIRD = 1.0 / 3.0
PIECE = 1024
HALF = DC * D
EP = E * 2 * HALF // PIECE
WRING = 4
HRING = 2 * WRING
KIB = 1024

C_ID, C_TRI, C_ONE, C_THR, C_REV, C_TIX, C_END = 0, 128, 256, 384, 416, 424, 424 + TILES


def piece_at(n, hc):
    if isinstance(n, int) and n < 2:
        half, m = HC // 2 * n, hc
    elif hc % 2 == 0:
        half, m = HC // 4 * (n + 2), hc // 2
    else:
        return None
    return half * 2 + m, half + m // 2, half + (m + 1) // 2, m % 2


def shared_moe_kernel(nc, xT, w0, condT, router_w, router_b, shared_w, expert_w, consts, tokid, padslots, padrows, out):
    ctx = ExitStack()
    with ctx:
        base = -(-nc.sbuf_base // 128) * 128

        def sb(name, shape, dt, kib):
            return nc.alloc_sbuf_tensor_at(name, [P] + shape, dt, offset=base + int(kib * KIB))

        def sem(name):
            return ctx.enter_context(nc.semaphore(name))

        x1t = sb("x1t", [2, DC, BLK], FP32, 0)
        w13h = sb("w13h", [HC, 2, DC, P], FP32R, 16)
        w13l = sb("w13l", [HC, 2, DC, P], FP32R, 48)
        wmh = sb("wmh", [2, DC, D], FP32R, 80)
        wml = sb("wml", [2, DC, D], FP32R, 96)
        w2h = wmh[:, :, :, :].rearrange("p b c n -> p (b c) n")
        w2l = wml[:, :, :, :].rearrange("p b c n -> p (b c) n")
        xin = sb("xin", [2, DC, BLK], FP32, 144)
        we = sb("we", [WRING, 2, 2, 2, DC // 2, D], FP32R, 0)
        ehl = sb("ehl", [2, 2, PIECE], FP32R, 0)
        eraw = sb("eraw", [2, 2, PIECE], FP32, 0)
        xh = sb("xh", [2, DC, BLK], FP32R, 128)
        xl = sb("xl", [2, DC, BLK], FP32R, 112)
        xg = sb("xg", [RING, D], FP32, 144)
        xgth = sb("xgth", [2, DC, P], FP32R, 152)
        xgtl = sb("xgtl", [2, DC, P], FP32R, 156)
        hid = sb("hid", [2, HE], FP32, 128)
        hidth = sb("hidth", [2, DC, P], FP32R, 132)
        hidtl = sb("hidtl", [2, DC, P], FP32R, 136)
        ys = sb("ys", [RING, D], FP32, 176)
        xs = sb("xs", [2, PAIR, D], FP32, 192)
        x1tok = sb("x1tok", [2, SUB, D], FP32, 160)
        w0sq = sb("w0sq", [DC, D], FP32, 160)
        xres = sb("xres", [SUB, D], FP32, 160)
        outst = sb("outst", [SUB, D], FP32, 168)
        idrw = sb("idrw", [DC, P + E], FP32, 176)
        condp = sb("condp", [DC, BATCH, E], FP32, 179)
        logp = sb("logp", [NT, DC, E], FP32, 180)
        gh = sb("gh", [2, BLK], FP32R, 176)
        gl = sb("gl", [2, BLK], FP32R, 180)
        w0s = sb("w0s", [DC, D], FP32, 184)
        sil = sb("sil", [2, BLK], FP32, 184)
        gm = sb("gm", [2, BLK], FP32, 188)
        wraw = sb("wraw", [2, 1024], FP32, 192)
        rt = sb("rt", [8, NT * E], FP32, 192)
        at = [200.0]

        def small(name, shape, dt=FP32):
            n = 1
            for s in shape:
                n *= s
            t = sb(name, shape, dt, at[0])
            at[0] += -(-n * 4 // 32) * 32 / KIB
            assert base + at[0] * KIB <= nc.sbuf_usable_end
            return t

        cst = small("cst", [C_END])
        ident, tri, ones = cst[:, C_ID:C_ID + P], cst[:, C_TRI:C_TRI + P], cst[:, C_ONE:C_ONE + P]
        rw = small("rw", [2 * DC, E])
        rb = small("rb", [E])
        cnd = small("cnd", [DC, BATCH])
        mod = small("mod", [DC, BATCH])
        modsq = small("modsq", [DC, BATCH])
        dvar = small("dvar", [DC, BATCH])
        dtmp = small("dtmp", [DC, BATCH])
        dsc = small("dsc", [DC, BATCH])
        rconst = small("rconst", [BATCH, E])
        score = small("score", [NT, E])
        tid = small("tid", [NT], INT32)
        rec = small("rec", [K, NT, 2], INT32)
        sadr = small("sadr", [K, NT], INT32)
        slot = small("slot", [PADDED, 2], INT32)
        turn_of = small("turn_of", [TILES], INT32)
        place_of = small("place_of", [TILES], INT32)
        loads = small("loads", [3, E], INT32)
        o8 = small("o8", [8, E])
        e8 = small("e8", [6, E])
        s32 = small("s32", [8, NT])
        six = [small(f"six{k}", [1], INT32) for k in range(RING)]

        pairs = [ctx.enter_context(nc.psum_tensor(f"banks{2 * i}", [P, 2, 512], FP32)) for i in range(4)]
        bank = [pairs[i // 2][:, i % 2, :] for i in range(8)]
        lin_ps, tok_ps, misc_ps = bank[0:2], pairs[1:3], bank[6]
        a_ps, b_ps, o_ps = bank[0:2], bank[2:4], bank[4:8]
        rank_ps = bank[0]
        xt_ps, h_ps, ht_ps, y_ps = bank[0:2], bank[2:4], bank[4:6], bank[6:8]

        def chunks(s):
            return tok_ps[s % 2][:, :, 0:2 * (P + E)].rearrange("p b (c n) -> p b c n", c=2)

        x1t_d = nc.dram_tensor("x1t_d", [NBLK, P, DC, BLK], FP32)
        x1_d = nc.dram_tensor("x1_d", [TOK + PADROWS, D], FP32)
        xs_d = nc.dram_tensor("xs_d", [SLOTS, D], FP32)
        we_d = nc.dram_tensor("we_d", [EP, P, 2, PIECE], FP32R)
        slots_d = nc.dram_tensor("slots_d", [SLOTS, 2], INT32)

        small_in = sem("small_in")
        cond_in = sem("cond_in")
        w0_in = [sem(f"w0_in{k}") for k in range(2)]
        pads_in = sem("pads_in")
        xin_in = [sem(f"xin_in{j}") for j in range(2)]
        wraw_in = [sem(f"wraw_in{j}") for j in range(2)]
        xh_ready, xl_ready = sem("xh_ready"), sem("xl_ready")
        wmh_ready, wml_ready = sem("wmh_ready"), sem("wml_ready")
        prep = sem("prep")
        misc_done = sem("misc_done")
        root = sem("root")
        lin_done = sem("lin_done")
        x1t_done = sem("x1t_done")
        tok_done = sem("tok_done")
        x1_done = sem("x1_done")
        x1t_out = [sem(f"x1t_out{j}") for j in range(2)]
        x1_out = [sem(f"x1_out{j}") for j in range(2)]
        w_high, w_split = sem("w_high"), sem("w_split")
        logit_done, score_done = sem("logit_done"), sem("score_done")
        ab_done, sil_done = sem("ab_done"), sem("sil_done")
        gm_done = sem("gm_done")
        gh_ready, gl_ready = sem("gh_ready"), sem("gl_ready")
        down_done, o_done = sem("down_done"), sem("o_done")
        xres_in, out_stored = sem("xres_in"), sem("out_stored")
        step = sem("step")
        mask_done, rank_mm, rank_done = sem("mask_done"), sem("rank_mm"), sem("rank_done")
        sadr_done, listed, slots_in, tables_done = sem("sadr_done"), sem("listed"), sem("slots_in"), sem("tables_done")
        er_in = [sem(f"er_in{j}") for j in range(2)]
        eh_ready, el_ready = sem("eh_ready"), sem("el_ready")
        ehl_out = [sem(f"ehl_out{j}") for j in range(2)]
        we_in = [sem(f"we_in{i}") for i in range(HRING)]
        weights_in = sem("weights_in")
        rows_in = [sem(f"rows_in{j}") for j in range(2)]
        staged = [sem(f"staged{j}") for j in range(2)]
        issue = sem("issue")
        ixc = sem("ixc")
        xg_in = [sem(f"xg_in{j}") for j in range(2)]
        tx_done, th_done, mm1_done, mm2_done = sem("tx_done"), sem("th_done"), sem("mm1_done"), sem("mm2_done")
        xgth_done, hidth_done = sem("xgth_done"), sem("hidth_done")
        xgt_done, hid_done, hidt_done = sem("xgt_done"), sem("hid_done"), sem("hidt_done")
        ys_done = sem("ys_done")
        added = sem("added")

        block = ctx.enter_context(nc.Block())

        @block.sync
        def _(sp):
            for j in range(2):
                sp.sem_inc(x1t_out[j], 16)
                sp.sem_inc(x1_out[j], 16)
                sp.sem_inc(ehl_out[j], 16)
            sp.dma_start(cnd[:, :, :], condT).then_inc(cond_in, 16)
            for k in range(2):
                sp.dma_start(w0s[:, :, k * D // 2:(k + 1) * D // 2], w0[:, :, k * D // 2:(k + 1) * D // 2]).then_inc(w0_in[k], 16)
            sp.dma_start(rw[:, :, :], router_w).then_inc(small_in, 16)
            sp.dma_start(xin[:, 0], xT[0]).then_inc(xin_in[0], 16)
            sp.dma_start(cst[:, :], consts).then_inc(small_in, 16)
            sp.dma_start(rb[:, :], router_b).then_inc(small_in, 16)
            sp.dma_start(tid[:, :], tokid).then_inc(small_in, 16)
            sp.dma_start(xin[:, 1], xT[1]).then_inc(xin_in[1], 16)
            for j in range(2):
                sp.dma_start(wraw[:, j, :], shared_w[j]).then_inc(wraw_in[j], 16)
            sp.dma_start(slots_d[:, :].rearrange("(p t) c -> p (t c)", p=P), padslots).then_inc(pads_in, 16)
            sp.dma_start(x1_d[TOK:TOK + PADROWS, :], padrows).then_inc(pads_in, 16)
            sp.dma_start(out[TOK:TOK + PADROWS, :], padrows).then_inc(pads_in, 16)

            for n in range(NBLK):
                j = n % 2
                sp.wait_ge(xh_ready, 4 * n + 4)
                sp.wait_ge(x1t_done, 4 * n + 4 + 2)
                if n < NBLK - 2:
                    sp.dma_start(xin[:, j], xT[n + 2]).then_inc(xin_in[j], 16)
                else:
                    sp.wait_ge(x1t_out[j], 16 + 16)
                    sp.dma_start(xin[:, j], x1t_d[j]).then_inc(xin_in[j], 16)
                sp.dma_start(x1t_d[n], x1t[:, j]).then_inc(x1t_out[j], 16)
                sp.wait_ge(w_split, n + 1)
                sp.dma_start(wraw[:, j, :], shared_w[n + 2]).then_inc(wraw_in[j], 16)
            for j in range(2):
                sp.wait_ge(w_split, NBLK + j + 1)
                sp.dma_start(wraw[:, j, :], shared_w[NBLK + 2 + j]).then_inc(wraw_in[j], 16)
            for j in range(2):
                sp.wait_ge(x1t_out[j], 16 * NBLK // 2 + 16)
                sp.wait_ge(x1_out[j], 16 * NBLK // 2 + 16)
            sp.wait_ge(tok_done, 4 * NBLK + 5)
            sp.dma_start(eraw[:, 0, 1], expert_w[0]).then_inc(er_in[0], 16)

            def load_res(n):
                sp.wait_ge(o_done, 4 * n)
                sp.dma_start(xres[:, :, :], x1_d[bass.ds(n * BLK, BLK), :].rearrange("(s p) d -> p s d", p=P)).then_inc(xres_in, 16)

            def store_out(n):
                sp.wait_ge(o_done, 4 * n + 4)
                sp.dma_start(out[bass.ds(n * BLK, BLK), :].rearrange("(s p) d -> p s d", p=P), outst[:, :, :]).then_inc(out_stored, 16)

            def load_x1t(n, j):
                sp.wait_ge(xh_ready, 4 * (NBLK + n + 1))
                sp.wait_ge(xl_ready, 4 * (NBLK + n + 1))
                sp.dma_start(xin[:, j], x1t_d[bass.ds(n + 2, 1)].rearrange("a p c t -> p (a c) t")).then_inc(xin_in[j], 16)

            def move_piece(n, hc):
                q, _, half, j = piece_at(n, hc)
                if q + 1 < EP:
                    sp.wait_ge(ehl_out[1 - j], 16 * half + 16)
                    sp.dma_start(eraw[:, 1 - j, 1], expert_w[q + 1]).then_inc(er_in[1 - j], 16)
                sp.wait_ge(el_ready, q + 1)
                sp.dma_start(we_d[q].rearrange("p s n -> p (s n)").bitcast(FP32), ehl[:, j].bitcast(FP32)).then_inc(ehl_out[j], 16)

            for n in range(NBLK - 2):
                for hc in range(HC):
                    if piece_at(n, hc):
                        move_piece(n, hc)
                    if hc == 1:
                        if n:
                            store_out(n - 1)
                        load_res(n)
                    if hc == 5:
                        load_x1t(n, n % 2)

            def table(row_, r, most):
                return sp.value_load(loads[0:1, row_, r:r + 1], min_val=0, max_val=most)

            def load_weight(i, e, place):
                sp.dma_start(we[:, place, i % 2].rearrange("p a h s c n -> p (a h) (s c n)").bitcast(FP32),
                             we_d[bass.ds(e * 4 + i % 2 * 2, 2)].rearrange("h p s n -> p h (s n)").bitcast(FP32)).then_inc(we_in[i % HRING], 16)

            def weight_loaded(i):
                sp.wait_ge(we_in[i % HRING], 16 * (i // HRING) + 16)
                sp.sem_inc(weights_in, 1)

            sp.wait_ge(tables_done, 3)
            first = [table(0, r, E - 1) for r in range(WRING)]
            for j in range(2):
                sp.wait_ge(ehl_out[j], 16 * EP // 2 + 16)
            load_weight(0, first[0], slice(0, 1))
            for n in (NBLK - 2, NBLK - 1):
                store_out(n - 1)
                load_res(n)
            weight_loaded(0)
            sp.wait_ge(ab_done, HC * NBLK)
            load_weight(1, first[0], slice(0, 1))
            store_out(NBLK - 1)
            weight_loaded(1)
            for i in range(2, HRING):
                load_weight(i, first[i // 2], slice(i // 2, i // 2 + 1))
                weight_loaded(i)
            for r in range(WRING, E):
                e, place, over = table(0, r, E - 1), table(1, r, WRING - 1), table(2, r, TILES)
                sp.wait_ge(mm2_done, over + 1)
                for i in (2 * r, 2 * r + 1):
                    load_weight(i, e, bass.ds(place, 1))
                    weight_loaded(i)
            sp.wait_ge(pads_in, 48)
            sp.wait_ge(out_stored, 16 * NBLK)
            sp.wait_ge(added, 16 * TILES)

        @block.tensor
        def _(pe):
            pe.sem_inc(lin_done, 1)
            pe.sem_inc(tok_done, 5)
            pe.sem_inc(mm2_done, 1)
            for o in range(DC):
                if o % 2 == 0:
                    pe.wait_ge(prep, 3 + o // 2)
                for c in range(DC):
                    last = pe.matmul(misc_ps[:, o * BATCH:(o + 1) * BATCH], w0sq[:, c, o * P:(o + 1) * P], modsq[:, c, :],
                                     start=(c == 0), stop=(c == DC - 1))
            last.then_inc(misc_done, 1)

            def condition_logits():
                pe.wait_ge(prep, 5)
                pe.wait_ge(small_in, 64)
                for c in range(DC):
                    last = pe.matmul(misc_ps[:, 16:16 + BATCH * E], ones, condp[:, c].rearrange("p b e -> p (b e)"),
                                     start=(c == 0), stop=(c == DC - 1))
                last.then_inc(misc_done, 1)

            def linear(n, wb, j):
                for o in range(DC):
                    pe.wait_ge(x1t_done, 4 * n + o + 1)
                    for c in range(DC):
                        if o == 0:
                            pe.wait_ge(xl_ready, 4 * n + c + 1)
                        w_hi, w_lo = wmh[:, wb, c, o * P:(o + 1) * P], wml[:, wb, c, o * P:(o + 1) * P]
                        pe.matmul(lin_ps[o % 2][:, :], w_hi, xh[:, j, c, :], start=(c == 0), stop=False)
                        pe.matmul(lin_ps[o % 2][:, :], w_hi, xl[:, j, c, :], start=False, stop=False)
                        last = pe.matmul(lin_ps[o % 2][:, :], w_lo, xh[:, j, c, :], start=False, stop=(c == DC - 1))
                    last.then_inc(lin_done, 1)

            def by_token(n, j):
                if n == 0:
                    pe.wait_ge(prep, 7)
                pe.wait_ge(x1t_done, 4 * n + DC + 2)
                for s in range(SUB):
                    pe.wait_ge(x1_done, 4 * n + s + 1)
                    for o in range(DC):
                        last = pe.matmul(tok_ps[s % 2][:, o // 2, o % 2 * (P + E):(o % 2 + 1) * (P + E)],
                                         x1t[:, j, o, s * P:(s + 1) * P], idrw[:, o, :], start=True, stop=True)
                    last.then_inc(tok_done, 1)

            for n in range(NBLK):
                if n % 2 == 0:
                    pe.wait_ge(wml_ready, DC * (n // 2 + 1))
                linear(n, n // 2 % 2, n % 2)
                if n:
                    by_token(n - 1, (n - 1) % 2)
                else:
                    condition_logits()
            by_token(NBLK - 1, 1)

            def up(n, hc, j):
                q = HC * n + hc
                if hc == 0:
                    pe.wait_ge(xl_ready, 4 * (NBLK + n + 1))
                pe.wait_ge(gm_done, q + 1)
                for ps, m in ((a_ps, 0), (b_ps, 1)):
                    for c in range(DC):
                        w_hi, w_lo = w13h[:, hc, m, c, :], w13l[:, hc, m, c, :]
                        pe.matmul(ps[hc % 2][:, :], w_hi, xh[:, j, c, :], start=(c == 0), stop=False)
                        pe.matmul(ps[hc % 2][:, :], w_hi, xl[:, j, c, :], start=False, stop=False)
                        last = pe.matmul(ps[hc % 2][:, :], w_lo, xh[:, j, c, :], start=False, stop=(c == DC - 1))
                last.then_inc(ab_done, 1)

            def down(n, hc):
                q = HC * n + hc
                pe.wait_ge(gl_ready, q + 1)
                if hc == 0:
                    pe.wait_ge(o_done, 4 * n)
                k = hc % 2
                for s in range(SUB):
                    g_hi, g_lo = gh[:, k, s * P:(s + 1) * P], gl[:, k, s * P:(s + 1) * P]
                    pe.matmul(o_ps[s][:, :], g_hi, w2h[:, hc, :], start=(hc == 0), stop=False)
                    pe.matmul(o_ps[s][:, :], g_hi, w2l[:, hc, :], start=False, stop=False)
                    last = pe.matmul(o_ps[s][:, :], g_lo, w2h[:, hc, :], start=False, stop=(hc == HC - 1))
                last.then_inc(down_done, 1)

            def shared_block(n, j):
                for hc in range(HC):
                    up(n, hc, j)
                    if hc:
                        down(n, hc - 1)
                    else:
                        down(n - 1, HC - 1)

            pe.wait_ge(w_split, HC)
            pe.wait_ge(x1t_done, DC * NBLK + 2)
            pe.wait_ge(x1_done, SUB * NBLK + 2)
            up(0, 0, 0)
            pe.wait_ge(logit_done, 1)
            for hc in range(1, HC):
                up(0, hc, 0)
                pe.wait_ge(w_split, HC + 1 + (hc - 1) // 2)
                down(0, hc - 1)
            for hc in range(HC):
                if hc == 5:
                    pe.wait_ge(mask_done, 1)
                    pe.wait_ge(gm_done, HC + 4 + 1 + 2)
                    pe.matmul(rank_ps[:, 0:NT * E], tri, rt[:, 4, :], start=True, stop=True)
                    pe.matmul(rank_ps[:, NT * E:2 * NT * E], ones, rt[:, 4, :], start=True, stop=True).then_inc(rank_mm, 1)
                if hc == 6:
                    pe.wait_ge(rank_done, 1)
                up(1, hc, 1)
                if hc:
                    down(1, hc - 1)
                else:
                    down(0, HC - 1)
            with pe.Fori(1, NBLK // 2) as h:
                for j in range(2):
                    shared_block(2 * h + j, j)

            def transpose_x(t, k, turn):
                if k % PAIR == 0:
                    pe.wait_ge(xg_in[k // PAIR % 2], 16 * turn + 16)
                pe.wait_ge(xgt_done, t + 1)
                for c in range(DC):
                    last = pe.transpose(xt_ps[k % 2][:, c * P:(c + 1) * P], xg[:, k % RING, c * P:(c + 1) * P], ident)
                last.then_inc(tx_done, 1)

            def transpose_h(t, k):
                pe.wait_ge(hid_done, t + 1 + 2)
                pe.wait_ge(hidt_done, t + 1)
                for c in range(DC):
                    last = pe.transpose(ht_ps[k % 2][:, c * P:(c + 1) * P], hid[:, k % 2, c * P:(c + 1) * P], ident)
                last.then_inc(th_done, 1)

            def product(ps, high, low, place, m):
                for c in range(DC):
                    w_hi, w_lo = (we[:, bass.ds(place, 1), m, c // 2, part, c % 2, :].rearrange("p a n -> p (a n)") for part in range(2))
                    pe.matmul(ps, high[:, c, :], w_hi, start=(c == 0), stop=False)
                    pe.matmul(ps, high[:, c, :], w_lo, start=False, stop=False)
                    last = pe.matmul(ps, low[:, c, :], w_hi, start=False, stop=(c == DC - 1))
                return last

            def expert_of(t):
                return (pe.value_load(turn_of[0:1, bass.ds(t, 1)], min_val=0, max_val=E - 1),
                        pe.value_load(place_of[0:1, bass.ds(t, 1)], min_val=0, max_val=WRING - 1))

            def matmul1(t, k):
                turn, place = expert_of(t)
                pe.wait_ge(weights_in, 2 * turn + 1)
                pe.wait_ge(xgt_done, t + 1 + 2)
                pe.wait_ge(hid_done, t + 1)
                product(h_ps[k % 2][:, :], xgth[:, k % 2], xgtl[:, k % 2], place, 0).then_inc(mm1_done, 1)

            def matmul2(t, k):
                turn, place = expert_of(t)
                pe.wait_ge(weights_in, 2 * turn + 2)
                pe.wait_ge(hidt_done, t + 1 + 2)
                pe.wait_ge(ys_done, t + 1)
                product(y_ps[k % 2][:, :], hidth[:, k % 2], hidtl[:, k % 2], place, 1).then_inc(mm2_done, 1)

            pe.wait_ge(tables_done, 3)
            pe.wait_ge(gm_done, HC * NBLK - 1 + 2)
            transpose_x(0, 0, 0)
            down(NBLK - 1, HC - 1)
            pe.wait_ge(gm_done, HC * NBLK + 2)
            matmul1(0, 0)
            transpose_x(1, 1, 0)
            pe.wait_ge(o_done, SUB * NBLK)
            transpose_h(0, 0)
            with pe.Fori(0, TURNS) as i:
                for k in range(1, RING + 1):
                    t = RING * i + k
                    matmul1(t, k)
                    transpose_x(t + 1, k + 1, i + (k + 1) // RING)
                    matmul2(t - 1, k - 1)
                    transpose_h(t, k)
            for t in range(RING * TURNS + 1, TILES):
                matmul1(t, t)
                if t + 1 < TILES:
                    transpose_x(t + 1, t + 1, (t + 1) // RING)
                matmul2(t - 1, t - 1)
                transpose_h(t, t)
            matmul2(TILES - 1, TILES - 1)

        @block.scalar
        def _(act):
            act.sem_inc(x1_done, 2)
            act.sem_inc(hid_done, 2)
            def x_high(j, c):
                act.activation(xh[:, j, c, :], xin[:, j, c, :], ACT.Copy).then_inc(xh_ready, 1)

            def weight_high(b):
                if b > 1:
                    act.wait_ge(lin_done, 2 * DC * (b - 1) + 1)
                for c in range(DC):
                    act.activation(wmh[:, b % 2, c, :], w0s[:, c, :], ACT.Copy,
                                   scale=mod[:, c, b:b + 1]).then_inc(wmh_ready, 1)

            def by_token(n, turn, j):
                act.wait_ge(x1_out[j], 16 * turn + 16)
                for s in range(SUB):
                    act.wait_ge(tok_done, 4 * n + s + 1 + 5)
                    act.activation(x1tok[:, j, s, :].rearrange("p (b c n) -> p b c n", b=2, c=2), chunks(s)[:, :, :, 0:P],
                                   ACT.Copy)
                    act.activation(logp[:, SUB * n + s].rearrange("p (b c) e -> p b c e", b=2), chunks(s)[:, :, :, P:P + E],
                                   ACT.Copy).then_inc(x1_done, 1)
                act.wait_ge(x1_done, SUB * n + SUB + 2)
                act.dma_start(x1_d[bass.ds(n * BLK, BLK), :].rearrange("(s p) d -> p s d", p=P), x1tok[:, j]).then_inc(x1_out[j], 16)

            for k in range(2):
                act.wait_ge(w0_in[k], 16)
            act.wait_ge(prep, 1)
            weight_high(0)
            act.wait_ge(xin_in[0], 16)
            for c in range(DC):
                x_high(0, c)
            act.wait_ge(prep, 6)
            act.activation(dtmp[:, :, :], dvar[:, :, :], ACT.Sqrt).then_inc(root, 1)
            for n in range(NBLK):
                act.wait_ge(xin_in[(n + 1) % 2], 16 * ((n + 1) // 2) + 16)
                act.wait_ge(lin_done, DC * n + 1)
                for c in range(DC):
                    x_high((n + 1) % 2, c)
                if n % 2 == 0 and n + 2 < NBLK:
                    weight_high(n // 2 + 1)
                act.wait_ge(wraw_in[n % 2], 16 * (n // 2) + 16)
                act.activation(w13h[:, n].rearrange("p m c n -> p (m c n)"), wraw[:, n % 2, :], ACT.Copy).then_inc(w_high, 1)
                if n:
                    by_token(n - 1, (n - 1) // 2, (n - 1) % 2)
            by_token(NBLK - 1, (NBLK - 1) // 2, 1)

            def w2_high(g):
                act.wait_ge(wraw_in[g % 2], 16 * ((HC + g) // 2) + 16)
                act.wait_ge(lin_done, DC * NBLK + 1)
                act.activation(w2h[:, 2 * g:2 * g + 2, :].rearrange("p b n -> p (b n)"), wraw[:, g % 2, :],
                               ACT.Copy).then_inc(w_high, 1)

            w2_high(0)
            act.wait_ge(logit_done, 1)
            act.activation(score[:, :, :], score[:, :, :], ACT.Sigmoid).then_inc(score_done, 1)

            def gate(n, hc):
                act.wait_ge(ab_done, HC * n + hc + 1)
                act.activation(sil[:, hc % 2, :], a_ps[hc % 2][:, :], ACT.Silu).then_inc(sil_done, 1)

            def hidden_high(n, hc):
                act.wait_ge(gm_done, HC * n + hc + 1 + 2)
                act.activation(gh[:, hc % 2, :], gm[:, hc % 2, :], ACT.Copy).then_inc(gh_ready, 1)

            def next_high(n, hc, j, turn):
                if hc == 2:
                    act.wait_ge(xin_in[(j + 1) % 2], 16 * turn + 16)
                    act.wait_ge(ab_done, HC * n)
                if 2 <= hc < 2 + DC:
                    x_high((j + 1) % 2, hc - 2)

            def piece_high(n, hc):
                if piece_at(n, hc):
                    _, half, _, j = piece_at(n, hc)
                    act.wait_ge(er_in[j], 16 * half + 16)
                    act.activation(ehl[:, j, 0], eraw[:, j, 1], ACT.Copy).then_inc(eh_ready, 1)

            def block_steps(n, j, turn, pieces=True):
                for hc in range(HC):
                    gate(n, hc)
                    if turn is not None:
                        next_high(n, hc, j, turn)
                    hidden_high(n, hc)
                    if pieces:
                        piece_high(n, hc)

            for hc in range(HC):
                gate(0, hc)
                next_high(0, hc, 0, NBLK // 2)
                hidden_high(0, hc)
                if hc in (0, 2, 4):
                    w2_high(1 + hc // 2)
                piece_high(0, hc)
            block_steps(1, 1, NBLK // 2 + 1)

            with act.Fori(1, NBLK // 2 - 1) as h:
                block_steps(2 * h, 0, NBLK // 2 + h)
                block_steps(2 * h + 1, 1, NBLK // 2 + h + 1)
            block_steps(NBLK - 2, 0, NBLK - 1, False)

            def load_rows(t, k, turn):
                j = k // PAIR % 2
                act.wait_ge(staged[j], 16 * turn + 16)
                act.dma_start(xg[:, k % RING:k % RING + PAIR, :],
                              xs_d[bass.ds(t * P, PAIR * P), :].rearrange("(t p) d -> p t d", p=P)).then_inc(xg_in[j], 16)

            act.wait_ge(xl_ready, DC * 2 * NBLK)
            load_rows(0, 0, 0)
            load_rows(PAIR, PAIR, 0)
            block_steps(NBLK - 1, 1, None, False)

            def take_x(t, k):
                act.wait_ge(tx_done, t + 1)
                act.activation(xgth[:, k % 2].rearrange("p c n -> p (c n)"), xt_ps[k % 2][:, :], ACT.Copy).then_inc(xgth_done, 1)

            def experts_step(t, k, turn, more=True, rows=True):
                act.wait_ge(mm1_done, t + 1)
                act.activation(hid[:, k % 2, :], h_ps[k % 2][:, :], ACT.Gelu).then_inc(hid_done, 1)
                if more:
                    take_x(t + 1, k + 1)
                    if k % PAIR == 0 and rows:
                        load_rows(t + RING, k, turn + 1)
                act.wait_ge(th_done, t + 1)
                act.activation(hidth[:, k % 2].rearrange("p c n -> p (c n)"), ht_ps[k % 2][:, :], ACT.Copy).then_inc(hidth_done, 1)

            take_x(0, 0)
            with act.Fori(0, TURNS) as i:
                for k in range(RING):
                    experts_step(RING * i + k, k, i)
            for t in range(RING * TURNS, TILES):
                experts_step(t, t, 0, t + 1 < TILES, False)

        @block.vector
        def _(dve):
            steps = [0]

            def then(ins):
                steps[0] += 1
                ins.then_inc(step, 1)
                dve.wait_ge(step, steps[0])

            dve.sem_inc(x1t_done, 2)
            dve.sem_inc(gm_done, 2)
            dve.sem_inc(xgt_done, 2)
            dve.sem_inc(hidt_done, 2)
            dve.sem_inc(ys_done, 2)
            dve.wait_ge(cond_in, 16)
            dve.tensor_scalar(mod[:, :, :], cnd[:, :, :], float(np.float32(1.0) / np.sqrt(np.float32(D))), None, ALU.mult).then_inc(prep, 1)
            dve.wait_ge(prep, 1)
            dve.tensor_tensor(modsq[:, :, :], mod[:, :, :], mod[:, :, :], ALU.mult).then_inc(prep, 1)
            for k in range(2):
                half = slice(k * D // 2, (k + 1) * D // 2)
                dve.wait_ge(w0_in[k], 16)
                dve.tensor_tensor(w0sq[:, :, half], w0s[:, :, half], w0s[:, :, half], ALU.mult).then_inc(prep, 1)

            def x_low(m, j, c):
                dve.wait_ge(xh_ready, DC * m + c + 1)
                dve.tensor_tensor(xl[:, j, c, :], xin[:, j, c, :], xh[:, j, c, :].bitcast(FP32), ALU.subtract).then_inc(xl_ready, 1)

            def weight_low(b, c):
                dve.wait_ge(wmh_ready, DC * b + c + 1)
                dve.scalar_tensor_tensor(wml[:, b % 2, c, :], w0s[:, c, :], mod[:, c, b:b + 1],
                                         wmh[:, b % 2, c, :].bitcast(FP32), ALU.mult, ALU.subtract).then_inc(wml_ready, 1)

            for c in range(DC):
                weight_low(0, c)
            for c in range(DC):
                x_low(0, 0, c)
            dve.wait_ge(small_in, 64)
            dve.tensor_tensor(condp[:, :, :, :], cnd[:, :, :].unsqueeze(3).to_broadcast([P, DC, BATCH, E]),
                              rw[:, DC:2 * DC, :].unsqueeze(2).to_broadcast([P, DC, BATCH, E]), ALU.mult).then_inc(prep, 1)
            dve.wait_ge(misc_done, 1)
            dve.tensor_scalar(dvar[:, :, :].rearrange("p c b -> p (c b)"), misc_ps[:, 0:DC * BATCH], EPS, None,
                              ALU.add).then_inc(prep, 1)
            dve.wait_ge(root, 1)
            then(dve.reciprocal(dsc[:, :, :], dtmp[:, :, :]))
            then(dve.tensor_tensor(dtmp[:, :, :], dsc[:, :, :], dsc[:, :, :], ALU.mult))
            then(dve.tensor_tensor(dtmp[:, :, :], dtmp[:, :, :], dvar[:, :, :], ALU.mult))
            then(dve.tensor_scalar(dtmp[:, :, :], dtmp[:, :, :], -0.5, 1.5, ALU.mult, ALU.add))
            then(dve.tensor_tensor(dsc[:, :, :], dsc[:, :, :], dtmp[:, :, :], ALU.mult))
            dve.tensor_copy(idrw[:, :, 0:P], ident.unsqueeze(1).to_broadcast([P, DC, P]))
            dve.tensor_copy(idrw[:, :, P:P + E], rw[:, 0:DC, :]).then_inc(prep, 1)

            for n in range(NBLK):
                j = n % 2
                for o in range(DC):
                    dve.wait_ge(lin_done, DC * n + o + 1 + 1)
                    if o == 0:
                        dve.wait_ge(x1t_out[j], 16 * (n // 2) + 16)
                        if n:
                            dve.wait_ge(tok_done, 4 * n - 4 + 5)
                    dve.scalar_tensor_tensor(x1t[:, j, o, :], lin_ps[o % 2][:, :], dsc[:, o, n // 2:n // 2 + 1],
                                             xin[:, j, o, :], ALU.mult, ALU.add).then_inc(x1t_done, 1)
                    if j == 0 and n + 2 < NBLK:
                        weight_low(n // 2 + 1, o)
                    for c in (range(o, o + 1) if n == 0 else ((), (), (0,), (1, 2, 3))[o]):
                        x_low(n + 1, (n + 1) % 2, c)
                dve.wait_ge(w_high, n + 1)
                w_hi = w13h[:, n].rearrange("p m c n -> p (m c n)").bitcast(FP32)
                dve.tensor_tensor(w13l[:, n].rearrange("p m c n -> p (m c n)"), wraw[:, j, :], w_hi, ALU.subtract).then_inc(w_split, 1)

            def w2_low(g):
                dve.wait_ge(w_high, HC + g + 1)
                dve.tensor_tensor(w2l[:, 2 * g:2 * g + 2, :].rearrange("p b n -> p (b n)"), wraw[:, g % 2, :],
                                  w2h[:, 2 * g:2 * g + 2, :].rearrange("p b n -> p (b n)").bitcast(FP32),
                                  ALU.subtract).then_inc(w_split, 1)

            w2_low(0)
            dve.wait_ge(misc_done, 2)
            dve.wait_ge(x1_done, SUB * NBLK + 2)
            then(dve.tensor_copy(rconst[:, :, :].rearrange("p b e -> p (b e)"), misc_ps[:, 16:16 + BATCH * E]))
            then(dve.tensor_tensor(logp[:, :, 0:2, :], logp[:, :, 0:2, :], logp[:, :, 2:4, :], ALU.add))
            then(dve.tensor_tensor(score[:, :, :], logp[:, :, 0, :], logp[:, :, 1, :], ALU.add))
            dve.tensor_tensor(score[:, :, :].rearrange("p (b t) e -> p b t e", b=BATCH),
                              score[:, :, :].rearrange("p (b t) e -> p b t e", b=BATCH),
                              rconst[:, :, :].unsqueeze(2).to_broadcast([P, BATCH, NT // BATCH, E]), ALU.add).then_inc(logit_done, 1)

            def product(n, hc):
                dve.wait_ge(sil_done, HC * n + hc + 1)
                dve.tensor_tensor(gm[:, hc % 2, :], sil[:, hc % 2, :], b_ps[hc % 2][:, :], ALU.mult).then_inc(gm_done, 1)

            def hidden_low(n, hc):
                dve.wait_ge(gh_ready, HC * n + hc + 1)
                dve.tensor_tensor(gl[:, hc % 2, :], gm[:, hc % 2, :], gh[:, hc % 2, :].bitcast(FP32), ALU.subtract).then_inc(gl_ready, 1)

            def output(n):
                dve.wait_ge(down_done, HC * (n + 1))
                dve.wait_ge(xres_in, 16 * (n + 1))
                dve.wait_ge(out_stored, 16 * n)
                for s in range(SUB):
                    dve.scalar_tensor_tensor(outst[:, s, :], o_ps[s][:, :], THIRD, xres[:, s, :], ALU.mult, ALU.add).then_inc(o_done, 1)

            def block_step(n, hc, j, more):
                product(n, hc)
                if more and 2 <= hc < 2 + DC:
                    x_low(NBLK + n + 1, (j + 1) % 2, hc - 2)
                hidden_low(n, hc)

            def row(r, shape=(NT, E), dt=None):
                v = rt[:, r, :] if dt is None else rt[:, r, :].bitcast(dt)
                return v.rearrange("p (a b) -> p a b", b=shape[1])

            def per_tile(v):
                return v.unsqueeze(2).to_broadcast([P, NT, E])

            def per_expert(v):
                return v.unsqueeze(1).to_broadcast([P, NT, E])

            SEL, KEY, CHOICE, MASK = 0, 1, (2, 3), 4
            rev = cst[:, C_REV:C_REV + E]

            def choose(k):
                then(dve.tensor_reduce(s32[:, 0, :], row(SEL), AX.X, ALU.max))
                then(dve.tensor_tensor(row(KEY), row(SEL), per_tile(s32[:, 0, :]), ALU.is_equal))
                then(dve.tensor_tensor(row(KEY), row(KEY), per_expert(rev), ALU.mult))
                then(dve.tensor_reduce(s32[:, 0, :], row(KEY), AX.X, ALU.max))
                then(dve.tensor_tensor(row(CHOICE[k]), row(KEY), per_tile(s32[:, 0, :]), ALU.is_equal))
                then(dve.tensor_tensor(row(KEY), score[:, :, :], row(CHOICE[k]), ALU.mult))
                then(dve.tensor_reduce(s32[:, 1 + k, :], row(KEY), AX.X, ALU.add))
                if k == 0:
                    then(dve.scalar_tensor_tensor(row(SEL), row(CHOICE[0]), -3.0e38, row(SEL), ALU.mult, ALU.add))

            def gates():
                then(dve.tensor_tensor(s32[:, 3, :], s32[:, 1, :], s32[:, 2, :], ALU.add))
                then(dve.tensor_scalar(s32[:, 4, :], s32[:, 3, :], 1e-9, None, ALU.add))
                then(dve.reciprocal(s32[:, 5, :], s32[:, 4, :]))
                then(dve.tensor_scalar(s32[:, 6, :], s32[:, 3, :], 1e-9, None, ALU.is_gt))
                then(dve.tensor_scalar(s32[:, 7, :], s32[:, 6, :], -1.0 / K, 1.0 / K, ALU.mult, ALU.add))
                then(dve.tensor_tensor(s32[:, 5, :], s32[:, 5, :], s32[:, 6, :], ALU.mult))
                for k in range(K):
                    then(dve.tensor_tensor(s32[:, 1 + k, :], s32[:, 1 + k, :], s32[:, 5, :], ALU.mult))
                    then(dve.tensor_tensor(s32[:, 1 + k, :], s32[:, 1 + k, :], s32[:, 7, :], ALU.add))
                    then(dve.tensor_scalar(rec[:, k, :, 1].bitcast(FP32), s32[:, 1 + k, :], THIRD, None, ALU.mult))
                    then(dve.tensor_copy(rec[:, k, :, 0], tid[:, :]))

            WITHIN, TOTAL, PING, PONG, POS = 0, 1, 5, 6, 7

            def scan_tiles():
                src = TOTAL
                for d, dst in ((1, PING), (2, PONG), (4, PING), (8, PONG), (16, PING)):
                    dve.tensor_copy(row(dst)[:, 0:d, :], row(src)[:, 0:d, :])
                    then(dve.tensor_tensor(row(dst)[:, d:NT, :], row(src)[:, d:NT, :], row(src)[:, 0:NT - d, :], ALU.add))
                    src = dst

            def first_slots():
                count = row(PING)[:, NT - 1, :]
                then(dve.tensor_tensor(row(PONG, (E, NT)), count.unsqueeze(2).to_broadcast([P, E, NT]),
                                       cst[:, C_THR:C_THR + NT].unsqueeze(1).to_broadcast([P, E, NT]), ALU.is_gt))
                then(dve.tensor_reduce(e8[:, 0, :], row(PONG, (E, NT)), AX.X, ALU.add))
                src = 0
                for d, dst in ((1, 1), (2, 2), (4, 1)):
                    dve.tensor_copy(e8[:, dst, 0:d], e8[:, src, 0:d])
                    then(dve.tensor_tensor(e8[:, dst, d:E], e8[:, src, d:E], e8[:, src, 0:E - d], ALU.add))
                    src = dst
                then(dve.tensor_tensor(e8[:, 3, :], e8[:, 1, :], e8[:, 0, :], ALU.subtract))
                then(dve.tensor_scalar(e8[:, 4, :], e8[:, 3, :], float(P), None, ALU.mult))
                then(dve.tensor_tensor(row(POS), row(PING), row(TOTAL), ALU.subtract))
                then(dve.tensor_tensor(row(POS), row(POS), row(WITHIN), ALU.add))
                then(dve.tensor_tensor(row(POS), row(POS), per_expert(e8[:, 4, :]), ALU.add))

            def slot_rows():
                for k in range(K):
                    pos = s32[:, 3, :].bitcast(INT32)
                    tile_, part = s32[:, 4, :].bitcast(INT32), s32[:, 5, :].bitcast(INT32)
                    then(dve.tensor_tensor(row(PONG), row(CHOICE[k]), row(POS), ALU.mult))
                    then(dve.tensor_reduce(s32[:, 0, :], row(PONG), AX.X, ALU.add))
                    then(dve.tensor_copy(pos, s32[:, 0, :]))
                    then(dve.tensor_single_scalar(tile_, pos, 7, ALU.logical_shift_right))
                    then(dve.tensor_single_scalar(part, pos, P - 1, ALU.bitwise_and))
                    dve.scalar_tensor_tensor(sadr[:, k, :], part, float(PADDED), tile_, ALU.mult, ALU.add).then_inc(sadr_done, 1)

            def turns():
                some, upto, place, last, turn = (o8[:, r, :] for r in (0, 1, 2, 3, 4))
                index = cst[:, C_TIX:C_TIX + E]
                then(dve.tensor_scalar(some, e8[:, 0, :], 0.5, None, ALU.is_gt))
                src = 0
                for d, dst in ((1, 2), (2, 3), (4, 1)):
                    dve.tensor_copy(o8[:, dst, 0:d], o8[:, src, 0:d])
                    then(dve.tensor_tensor(o8[:, dst, d:E], o8[:, src, d:E], o8[:, src, 0:E - d], ALU.add))
                    src = dst
                used = o8[:, 1, E - 1:E]
                then(dve.tensor_tensor(turn, index, upto, ALU.subtract))
                then(dve.tensor_scalar(turn, turn, used, None, ALU.add))
                then(dve.scalar_tensor_tensor(last, upto, -1.0, turn, ALU.add, ALU.subtract))
                then(dve.tensor_tensor(last, last, some, ALU.mult))
                then(dve.tensor_tensor(turn, turn, last, ALU.add))
                then(dve.tensor_scalar(last, index, used, None, ALU.min))
                then(dve.tensor_scalar(place, last, float(WRING), float(-WRING), ALU.is_ge, ALU.mult))
                then(dve.tensor_tensor(place, place, last, ALU.add))
                dve.tensor_copy(loads[:, 1, :], place)
                match = rt[:, PING, 0:E * E].rearrange("p (a b) -> p a b", b=E)

                def pick(row_, wanted, values):
                    then(dve.tensor_tensor(match, turn.unsqueeze(1).to_broadcast([P, E, E]),
                                           wanted.unsqueeze(2).to_broadcast([P, E, E]), ALU.is_equal))
                    then(dve.tensor_tensor(match, match, values.unsqueeze(1).to_broadcast([P, E, E]), ALU.mult))
                    then(dve.tensor_reduce(o8[:, 5, :], match, AX.X, ALU.add))
                    return dve.tensor_copy(loads[:, row_, :], o8[:, 5, :])

                then(pick(0, last, index))
                then(dve.tensor_scalar(last, last, float(-WRING), None, ALU.add))
                pick(2, last, e8[:, 1, :]).then_inc(tables_done, 1)

            def tile_tables():
                then(dve.tensor_scalar(o8[:, 7, :], o8[:, 0, :], -2.0 * TILES, 2.0 * TILES, ALU.mult, ALU.add))
                then(dve.tensor_tensor(o8[:, 7, :], o8[:, 7, :], e8[:, 1, :], ALU.add))
                then(dve.tensor_scalar(o8[:, 6, :], o8[:, 1, :], -1.0, None, ALU.add))
                cmp_ = rt[0:1, PING:PING + 3, :].rearrange("p a b -> p (a b)")[:, 0:TILES * E].rearrange("p (t e) -> p t e", e=E)
                then(dve.tensor_tensor(cmp_, o8[0:1, 7, :].unsqueeze(1).to_broadcast([1, TILES, E]),
                                       cst[0:1, C_TIX:C_TIX + TILES].unsqueeze(2).to_broadcast([1, TILES, E]), ALU.is_le))
                turn, place = rt[0:1, WITHIN, 0:TILES], rt[0:1, TOTAL, 0:TILES]
                then(dve.tensor_reduce(turn, cmp_, AX.X, ALU.add))
                then(dve.tensor_scalar(turn, turn, o8[0:1, 6, E - 1:E], None, ALU.min))
                dve.tensor_copy(turn_of[0:1, :], turn).then_inc(tables_done, 1)
                then(dve.tensor_scalar(place, turn, float(WRING), float(-WRING), ALU.is_ge, ALU.mult))
                dve.tensor_tensor(place_of[0:1, :], place, turn, ALU.add).then_inc(tables_done, 1)

            def piece_low(n, hc):
                if piece_at(n, hc):
                    q, _, _, j = piece_at(n, hc)
                    dve.wait_ge(eh_ready, q + 1)
                    dve.tensor_tensor(ehl[:, j, 1], eraw[:, j, 1], ehl[:, j, 0].bitcast(FP32), ALU.subtract).then_inc(el_ready, 1)

            for hc in range(HC):
                block_step(0, hc, 0, True)
                if hc in (0, 2, 4):
                    w2_low(1 + hc // 2)
                if hc == 5:
                    dve.wait_ge(score_done, 1)
                    then(dve.tensor_tensor(row(SEL), score[:, :, :], per_expert(rb[:, :]), ALU.add))
                if hc == 6:
                    choose(0)
                if hc == 7:
                    choose(1)
                piece_low(0, hc)
            for hc in range(HC):
                block_step(1, hc, 1, True)
                if hc == 0:
                    output(0)
                if hc == 1:
                    dve.tensor_tensor(row(MASK), row(CHOICE[0]), row(CHOICE[1]), ALU.add).then_inc(mask_done, 1)
                    gates()
                if hc == 4:
                    dve.wait_ge(rank_mm, 1)
                    then(dve.tensor_copy(rt[:, WITHIN:TOTAL + 1, :].rearrange("p a b -> p (a b)"), rank_ps[:, :]))
                    dve.sem_inc(rank_done, 1)
                    scan_tiles()
                if hc == 5:
                    first_slots()
                if hc == 6:
                    slot_rows()
                if hc == 7:
                    turns()
                    tile_tables()
                piece_low(1, hc)
            with dve.Fori(1, NBLK // 2 - 1) as h:
                for j in range(2):
                    for hc in range(HC):
                        block_step(2 * h + j, hc, j, True)
                        if hc == 0:
                            output(2 * h + j - 1)
                        piece_low(2 * h + j, hc)
            for n in (NBLK - 2, NBLK - 1):
                for hc in range(HC):
                    block_step(n, hc, n % 2, n < NBLK - 1)
                    if hc == 0:
                        output(n - 1)
            def take_x(t, k):
                dve.wait_ge(xgth_done, t + 1)
                dve.tensor_tensor(xgtl[:, k % 2].rearrange("p c n -> p (c n)"), xt_ps[k % 2][:, :],
                                  xgth[:, k % 2].rearrange("p c n -> p (c n)").bitcast(FP32), ALU.subtract).then_inc(xgt_done, 1)

            def take_h(t, k):
                dve.wait_ge(hidth_done, t + 1)
                dve.tensor_tensor(hidtl[:, k % 2].rearrange("p c n -> p (c n)"), ht_ps[k % 2][:, :],
                                  hidth[:, k % 2].rearrange("p c n -> p (c n)").bitcast(FP32), ALU.subtract).then_inc(hidt_done, 1)

            def take_y(t, k, reused=True):
                dve.wait_ge(mm2_done, t + 1 + 1)
                if reused:
                    dve.wait_ge(added, 16 * (t + 1 - RING))
                dve.tensor_scalar(ys[:, k % RING, :], y_ps[k % 2][:, :], slot[:, bass.ds(t, 1), 1].bitcast(FP32), None,
                                  ALU.mult).then_inc(ys_done, 1)

            take_x(0, 0)
            output(NBLK - 1)
            dve.wait_ge(slots_in, 16)
            take_x(1, 1)
            take_h(0, 0)
            for t in range(1, RING + 1):
                take_x(t + 1, t + 1)
                take_y(t - 1, t - 1, False)
                take_h(t, t)
            with dve.Fori(1, TURNS) as i:
                for k in range(1, RING + 1):
                    t = RING * i + k
                    take_x(t + 1, k + 1)
                    take_y(t - 1, k - 1)
                    take_h(t, k)
            for t in range(RING * TURNS + 1, TILES):
                if t + 1 < TILES:
                    take_x(t + 1, t + 1)
                take_y(t - 1, t - 1)
                take_h(t, t)
            take_y(TILES - 1, TILES - 1)

        @block.gpsimd
        def _(pool):
            IO = bass.IndirectOffsetOnAxis
            pool.wait_ge(pads_in, 48)
            for k in range(K):
                pool.wait_ge(sadr_done, k + 1)
                for i in range(NT):
                    pool.indirect_dma_start(slots_d[:, :], IO(sadr[:, k, i:i + 1], 0), rec[:, k, i, :], None).then_inc(listed, 16)

            pool.wait_ge(listed, 16 * K * NT)
            pool.dma_start(slot[:, :, :], slots_d[:, :].rearrange("(p t) c -> p t c", p=P)).then_inc(slots_in, 16)
            pool.wait_ge(slots_in, 16)
            pool.wait_ge(tables_done, 3)
            for j in range(2):
                pool.wait_ge(x1_out[j], 16 * NBLK // 2 + 16)

            def store_rows(g):
                pool.wait_ge(rows_in[g % 2], 16 * PAIR * (g // 2 + 1))
                pool.dma_start(xs_d[g * PAIR * P:(g + 1) * PAIR * P, :].rearrange("(t p) d -> p t d", p=P),
                               xs[:, g % 2]).then_inc(staged[g % 2], 16)

            for g in range(PADDED // PAIR):
                if g >= 2:
                    pool.wait_ge(staged[g % 2], 16 * (g // 2))
                for k in range(PAIR):
                    t = g * PAIR + k
                    pool.indirect_dma_start(xs[:, g % 2, k, :], None, x1_d[:, :], IO(slot[:, t, 0:1], 0)).then_inc(rows_in[g % 2], 16)
                if g:
                    store_rows(g - 1)
            store_rows(PADDED // PAIR - 1)

            def scatter(t, k, copies):
                if not isinstance(t, int) or t:
                    pool.wait_ge(added, 16 * t)
                pool.tensor_copy(six[k][:, :], slot[:, bass.ds(t, 1), 0]).then_inc(ixc, 1)
                pool.wait_ge(ys_done, t + 1 + 2)
                pool.wait_ge(ixc, copies)
                pool.sem_inc(issue, 1)
                pool.indirect_dma_start(out[:, :], IO(six[k][:, :], 0), ys[:, k, :], None,
                                        compute_op=ALU.add).then_inc(added, 16)

            pool.wait_ge(out_stored, 16 * NBLK)
            for t in range(RING):
                scatter(t, t, t + 1)
            with pool.Fori(1, TURNS) as i:
                for k in range(RING):
                    scatter(RING * i + k, k, RING * i + k + 1)
            for t in range(RING * TURNS, TILES):
                scatter(t, t % RING, t + 1)


def _by_partition(a, chunks):
    a = a.reshape(*a.shape[:-2], chunks, P, a.shape[-1])
    return np.ascontiguousarray(np.swapaxes(a, -3, -2))


def _constants():
    c = np.zeros((P, C_END), np.float32)
    c[:, C_ID:C_ID + P] = np.eye(P)
    c[:, C_TRI:C_TRI + P] = np.triu(np.ones((P, P)), 1)
    c[:, C_ONE:C_ONE + P] = 1.0
    c[:, C_THR:C_THR + NT] = P * np.arange(NT)
    c[:, C_REV:C_REV + E] = E - np.arange(E)
    c[:, C_TIX:C_TIX + TILES] = np.arange(TILES)
    tokid = (P * np.arange(NT)[None, :] + np.arange(P)[:, None]).astype(np.int32)
    pads = np.zeros((P, PADDED, 2), np.int32)
    pads[:, :, 0] = TOK + np.arange(P)[:, None]
    return c, tokid, pads.reshape(P, 2 * PADDED)


def kernel(**inputs):
    import concourse.bacc as bacc
    from concourse.bass_utils import run_bass_kernel_spmd

    a = {k: np.asarray(v) for k, v in inputs.items()}
    xT = a["x"].reshape(NBLK, BLK, D).transpose(0, 2, 1)
    w13 = np.stack([a["L1_cond_w1"], a["L1_cond_w3"]]).reshape(2, DC, P, HC, P).transpose(3, 2, 0, 1, 4)
    w2 = a["L1_cond_w2"].reshape(HC // 2, 2, P, D).transpose(0, 2, 1, 3)
    experts = np.stack([_by_partition(a["L1_cond_W1e"], DC), _by_partition(a["L1_cond_W2e"], DC)], axis=1)
    experts = experts.reshape(2 * E, P, HALF // PIECE, PIECE).swapaxes(1, 2).reshape(EP, P, PIECE)
    consts, tokid, pads = _constants()
    arrays = {
        "xT": _by_partition(xT, DC),
        "w0": _by_partition(a["L0_cond_weight"], DC),
        "condT": _by_partition(a["cond_1024"].T, DC),
        "router_w": _by_partition(a["L1_cond_router_W"], 2 * DC),
        "router_b": np.ascontiguousarray(np.broadcast_to(a["L1_cond_router_bias"], (P, E))),
        "shared_w": np.concatenate([w13.reshape(HC, P, 1024), w2.reshape(HC // 2, P, 1024)]),
        "expert_w": np.ascontiguousarray(experts),
        "consts": consts,
        "tokid": tokid,
        "padslots": pads,
        "padrows": np.zeros((PADROWS, D), np.float32),
    }
    nc = bacc.Bacc("TRN2", target_bir_lowering=False, num_devices=1)
    args = {n: nc.dram_tensor(n, v.shape, mybir.dt.from_np(v.dtype), kind="ExternalInput").ap() for n, v in arrays.items()}
    out = nc.dram_tensor("out", (TOK + PADROWS, D), FP32, kind="ExternalOutput").ap()
    shared_moe_kernel(nc, **args, out=out)
    r = run_bass_kernel_spmd(nc, [arrays], core_ids=[0])
    return r.results[0]["out"][:TOK].reshape(BATCH, SEQ, D)
```
